# Optimizing a Trainium2 kernel written in Bass

```python
import numpy as np
import jax
import jax.numpy as jnp

def _softmax(x, axis=-1):
    return jax.nn.softmax(x, axis=axis)

def _gelu(x):
    return jax.nn.gelu(x, approximate=True)

def _silu(x):
    return jax.nn.silu(x)

def _sigmoid(x):
    return jax.nn.sigmoid(x)

def _layernorm(x, axis=-1, eps=1e-05):
    m = jnp.mean(x, axis=axis, keepdims=True)
    v = jnp.var(x, axis=axis, keepdims=True)
    return (x - m) / jnp.sqrt(v + eps)

def _scatter_add(tgt, idx, src, axis=0):
    return tgt.at[idx].add(src)

def _segment_sum(src, seg, n):
    return jax.ops.segment_sum(src, seg, n)
kernel_name = 'mk_conv_preact_d1_conv_nhwc384_r2_e948ff'

def setup_inputs(seed: int=0):
    np.random.seed(seed)
    _w = jnp.asarray

    def _rec_inputs():
        import jax
        import jax.numpy as jnp
        _gk = jax.random.key(seed)
        x = -9.26e-05 + 0.9999 * jax.random.normal(jax.random.fold_in(_gk, 1), (1, 128, 192, 192), jnp.float32)
        return x
    x = _rec_inputs()

    def _L0_conv_setup():
        import jax, jax.numpy as jnp
        import numpy as np
        N_HEAD = 12
        SCALING = 0.17677669529663687
        key = jax.random.key(seed)
        ks = jax.random.split(key, 6)
        B, R, C, E = (1, 128, 192, 192)
        s = 1.0 / np.sqrt(E)
        return {'x': jax.random.normal(ks[0], (B, R, C, E), dtype=jnp.float32), 'Wq': jax.random.normal(ks[1], (E, E), dtype=jnp.float32) * s, 'Wk': jax.random.normal(ks[2], (E, E), dtype=jnp.float32) * s, 'Wv': jax.random.normal(ks[3], (E, E), dtype=jnp.float32) * s, 'Wq_s': jax.random.normal(ks[4], (E, E), dtype=jnp.float32) * s, 'Wk_s': jax.random.normal(ks[5], (E, E), dtype=jnp.float32) * s, 'res_mask': jnp.ones((B, C), dtype=jnp.int32), 'seq_mask': jnp.ones((B, R), dtype=jnp.int32)}
    _L0_conv_all = _L0_conv_setup()
    _L0_conv_in = {k: v for k, v in _L0_conv_all.items() if k in ('Wq', 'Wk', 'Wv', 'Wq_s', 'Wk_s', 'res_mask', 'seq_mask')}
    del _L0_conv_all
    return {'x': x, 'L0_conv_Wq': _L0_conv_in['Wq'], 'L0_conv_Wk': _L0_conv_in['Wk'], 'L0_conv_Wv': _L0_conv_in['Wv'], 'L0_conv_Wq_s': _L0_conv_in['Wq_s'], 'L0_conv_Wk_s': _L0_conv_in['Wk_s'], 'L0_conv_res_mask': _L0_conv_in['res_mask'], 'L0_conv_seq_mask': _L0_conv_in['seq_mask']}

def reference(x, L0_conv_Wq, L0_conv_Wk, L0_conv_Wv, L0_conv_Wq_s, L0_conv_Wk_s, L0_conv_res_mask, L0_conv_seq_mask):
    import jax
    import jax.numpy as jnp

    def _L0_conv_ref(x, Wq, Wk, Wv, Wq_s, Wk_s, res_mask, seq_mask):
        import jax, jax.numpy as jnp
        import numpy as np
        N_HEAD = 12
        SCALING = 0.17677669529663687
        B, R, C, E = x.shape
        H = N_HEAD
        D = E // H
        NEG = jnp.finfo(x.dtype).min
        scale_s = 1.0 / np.sqrt(D)
        msa = jnp.transpose(x, (0, 2, 1, 3))
        q0 = msa[:, :, 0]
        Qs = (q0 @ Wq_s).reshape(B, C, 1, H, D)
        Qs = jnp.transpose(Qs, (0, 1, 3, 2, 4)) * scale_s
        Ks = (msa @ Wk_s).reshape(B, C, R, H, D)
        Ks = jnp.transpose(Ks, (0, 1, 3, 4, 2))
        QKs = Qs @ Ks
        QKs = jnp.where(seq_mask[:, None, None, None, :] == 0, NEG, QKs)
        sw = jax.nn.softmax(QKs, axis=-1)
        sw = jnp.transpose(sw, (0, 4, 1, 2, 3))
        scaling = SCALING / np.sqrt(C)
        Q = (x @ Wq).reshape(B, R, C, H, D) * scaling * sw
        K = (x @ Wk).reshape(B, R, C, H, D)
        V = (x @ Wv).reshape(B, R, C, H, D)
        QK = jnp.einsum('brihd,brjhd->bhij', Q, K)
        rm = res_mask[:, :, None] * res_mask[:, None, :]
        QK = jnp.where(rm[:, None, :, :] == 0, NEG, QK)
        attn = jax.nn.softmax(QK, axis=-1)
        out = jnp.einsum('bhij,brjhd->brihd', attn, V)
        return out.reshape(B, R, C, E)

    def _gn(v, G=32, eps=1e-05):
        B_, H_, W_, C_ = v.shape
        g = v.reshape(B_, H_, W_, G, C_ // G)
        m = jnp.mean(g, axis=(1, 2, 4), keepdims=True)
        s = jnp.var(g, axis=(1, 2, 4), keepdims=True)
        return ((g - m) / jnp.sqrt(s + eps)).reshape(v.shape)

    def _ln_c(v, eps=1e-06):
        m = jnp.mean(v, axis=-1, keepdims=True)
        s = jnp.var(v, axis=-1, keepdims=True)
        return (v - m) / jnp.sqrt(s + eps)

    def _ln_t(v, eps=1e-05):
        m = jnp.mean(v, axis=-1, keepdims=True)
        s = jnp.var(v, axis=-1, keepdims=True)
        return (v - m) / jnp.sqrt(s + eps)

    def _to_tokens(v):
        B_, H_, W_, C_ = v.shape
        return v.reshape(B_, H_ * W_, C_)

    def _from_tokens(t, like):
        return t.reshape(like.shape)
    x = x + _L0_conv_ref(_gn(x), L0_conv_Wq, L0_conv_Wk, L0_conv_Wv, L0_conv_Wq_s, L0_conv_Wk_s, L0_conv_res_mask, L0_conv_seq_mask)
    return x

_drawn_inputs = setup_inputs


def setup_inputs(seed=0):
    import zlib

    import numpy as np

    out = dict(_drawn_inputs(seed))
    spreads = {}
    factors = {'L0_conv_Wq': 8.0, 'L0_conv_Wk': 8.0, 'L0_conv_Wq_s': 8.0, 'L0_conv_Wk_s': 8.0}
    for name, (base, spread) in spreads.items():
        noise = np.random.default_rng([zlib.crc32(name.encode()), seed]).standard_normal(out[name].shape)
        drawn = base * np.exp(spread * noise) if base else spread * noise
        out[name] = jnp.asarray(drawn.astype(out[name].dtype))
    for name, factor in factors.items():
        out[name] = (out[name] * factor).astype(out[name].dtype)
    return out
```

```python
import concourse.bass as bass
from concourse import mybir
from contextlib import ExitStack

fp32 = mybir.dt.float32
fp16 = mybir.dt.float16
int32 = mybir.dt.int32
ALU = mybir.AluOpType
ACT = mybir.ActivationFunctionType
AX = mybir.AxisListType

R, C, E, H = 128, 192, 192, 12
D = E // H
G, GC = 32, E // 32
P = 128
E1 = E - P
HALF = H // 2
EH = HALF * D
FMAX = 3.4028234663852886e38
EPS = 1e-5
U_SCALE = 0.125
SW_SCALE = 2.0
CI = 8
SI = 2
NCH = C // CI
XC = 32
NXC = C // XC
WQ, WK, WV, WQS, WKS = range(5)


def row_column_attention(nc, x, wq, wk, wv, wqs, wks, res_mask, seq_mask, out):
    xs = x.rearrange("b r c e -> (b r) c e")
    outs = out.rearrange("b r c e -> (b r) c e")

    xt_dram = nc.dram_tensor("xt_scratch", [NCH, P, 3 * CI * R], fp16, kind="Internal").ap()
    v0_dram = nc.dram_tensor("v0_scratch", [2, P, R, 2 * EH], fp16, kind="Internal").ap()
    v1_dram = nc.dram_tensor("v1_scratch", [2, 2, E1, R, EH], fp16, kind="Internal").ap()

    ctx = ExitStack()
    with ctx:
        def sb(name, shape, dt=fp32):
            return ctx.enter_context(nc.sbuf_tensor(name, shape, dt))

        def sem(name):
            return ctx.enter_context(nc.semaphore(name))

        BIG = sb("BIG", [P, C * E])
        X = BIG[:, :]
        AR = C * E // 2
        QA = BIG[:, 0:AR].bitcast(fp16).rearrange("p (m s) -> p m s", s=2 * C)
        KA = BIG[:, AR:2 * AR].bitcast(fp16).rearrange("p (m s) -> p m s", s=2 * C)
        V0 = BIG[:, 0:P * EH].bitcast(fp16).rearrange("p (r s) -> p r s", s=2 * EH)
        V1 = BIG[:, P * EH:AR].bitcast(fp16).rearrange("p (r s) -> p r s", s=EH)
        XO = BIG[:, AR:2 * AR].rearrange("p (i e) -> p i e", e=EH)

        EXTRA = sb("EXTRA", [P, 10752])
        place = [0]

        def part(n):
            place[0] += n
            return EXTRA[:, place[0] - n:place[0]]

        UH0, UL0, UH1, UL1 = (part(C * H // 2).bitcast(fp16) for _ in range(4))
        after_u = place[0]
        XN = [part(CI * E).rearrange("p (t n) -> p t n", t=3) for _ in range(2)]
        TT = [part(CI * E).bitcast(fp16).rearrange("p (t s n) -> p t s n", t=3, s=2) for _ in range(2)]
        place[0] = after_u
        W = part(5 * 2 * E).rearrange("p (w t n) -> p w t n", w=5, t=2)
        ST = part(G * NXC * 6).rearrange("p (g c s) -> p g c s", g=G, c=NXC)
        WKT = part(2 * 256).rearrange("p (t n) -> p t n", t=2)
        QM = part(4 * C).rearrange("p (t a n) -> p t a n", t=2, a=2)
        X0 = part(2 * E).rearrange("p (t n) -> p t n", t=2)
        QX = part(2 * C).rearrange("p (t n) -> p t n", t=2)
        AB = part(2 * 256).rearrange("p (t n) -> p t n", t=2)
        row_i = part(C).bitcast(int32)
        place[0] = 0
        XT = [part(3 * CI * R // 2).bitcast(fp16) for _ in range(2)]
        VS = [part(CI * EH).bitcast(fp16).rearrange("p (i s) -> p i s", s=2 * EH) for _ in range(2)]
        TQ = [part(SI * EH).rearrange("p (m i) -> p m i", i=SI) for _ in range(4)]
        AT = part(HALF * 2 * C).bitcast(fp16).rearrange("p (h s n) -> p h s n", h=HALF, s=2)
        LG = [part(2 * 256).rearrange("p (t n) -> p t n", t=2) for _ in range(2)]
        LLOW = [part(C) for _ in range(2)]

        SW = sb("SW", [P, C * H])
        DM = SW[:, 0:G * 2 * NXC].rearrange("p (g k) -> p g k", g=G)
        WP = sb("WP", [P, 2, 2, 2, 3 * EH], fp16)
        ident = sb("ident", [P, P])
        ones = sb("ones", [P, P])
        M01 = sb("M01", [P, 2, C])
        NEG = sb("NEG", [P, 2, C])
        small = sb("small", [P, 512])
        sp = [0]

        def col(n):
            sp[0] += n
            return small[:, sp[0] - n:sp[0]]

        seq_i = sb("seq_i", [P, 1], int32)
        res_i = sb("res_i", [P, 2], int32)
        seq01, seqneg, seqscale = col(1), col(1), col(1)
        res01 = col(2)
        parity = col(2)
        mx5, m5t, mxb, rv5, d5 = col(5), col(1), col(5), col(5), col(5)
        alpha = col(1)
        s1, mean, s2, s3, var, y, t_n, y2 = (col(G) for _ in range(8))
        abc = col(6)
        smx, ssum, sinv = col(18), col(18), col(18)
        lmx, lsum, linv = col(2), col(2), col(2)
        row01 = M01[:, 1, :]

        PS = ctx.enter_context(nc.psum_tensor("PS", [P, 8, 512], fp32))

        s_x = [sem(f"x_loaded{c}") for c in range(NXC)]
        s_params = sem("params_loaded")
        STORES = 16 * 7
        N_PARAMS = 5 * 3 + 2 + 4
        s_zero = sem("tiles_zeroed")
        s_const = sem("constants_ready")
        s_dve = sem("vector_step")
        s_wmax = sem("weight_max_ready")
        s_wmaxT = sem("weight_max_transposed")
        s_wd = sem("weight_max_diagonal")
        s_wb = sem("weight_max_everywhere")
        s_wsc = sem("weights_scaled")
        s_wh = sem("weight_highs_ready")
        s_wkt = sem("wks_and_x0_transposed")
        s_st1 = sem("row_means_summed")
        s_mm1 = sem("means_added")
        s_st2 = sem("squares_summed")
        s_mm2 = sem("squares_added")
        s_var = sem("variance_ready")
        s_std = sem("deviation_ready")
        s_ab = sem("scale_shift_rows")
        s_abT = sem("scale_shift_columns_psum")
        s_x0n = sem("x0_normalised")
        s_qs = sem("row_queries_psum")
        s_qm = sem("row_queries_masked")
        s_u = sem("score_vectors_psum")
        s_uh = sem("score_vector_highs")
        s_ul = sem("score_vectors_split")
        s_tr = sem("x_transposed")
        s_xn = sem("xnT_ready")
        s_h = sem("xnT_highs")
        s_l = sem("xnT_lows")
        s_sp = [sem(f"xnT_stored{b}") for b in range(2)]
        s_sc = sem("scores_psum")
        s_se = sem("scores_ready")
        s_stt = sem("scores_transposed")
        s_ssh = sem("scores_shifted")
        s_sex = sem("scores_exponent")
        s_snm = sem("row_weights_normalised")
        s_swt = sem("row_weights_psum")
        s_sw = sem("row_weights_ready")
        s_xt = [[sem(f"xt{h}_loaded{b}") for b in range(2)] for h in range(2)]
        s_pj = [sem(f"projected{h}") for h in range(2)]
        s_kvh = [sem(f"kv_highs{h}") for h in range(2)]
        s_kvl = [sem(f"kv_lows{h}") for h in range(2)]
        s_tq = [sem(f"weighted_q{h}") for h in range(2)]
        s_qh = [sem(f"q_highs{h}") for h in range(2)]
        s_ql = [sem(f"q_lows{h}") for h in range(2)]
        s_vs = [[sem(f"v{h}_stored{b}") for b in range(2)] for h in range(2)]
        s_qk = [sem(f"logits_psum{h}") for h in range(2)]
        s_ll = [sem(f"logits_low_part{h}") for h in range(2)]
        s_lr = [sem(f"logits_read{h}") for h in range(2)]
        s_ls = [sem(f"logits_shifted{h}") for h in range(2)]
        s_le = [sem(f"logits_exponent{h}") for h in range(2)]
        s_at = [sem(f"attention_ready{h}") for h in range(2)]
        s_att = [sem(f"attention_transposed{h}") for h in range(2)]
        s_ath = [sem(f"attention_highs{h}") for h in range(2)]
        s_atl = [sem(f"attention_lows{h}") for h in range(2)]
        s_vl = [sem(f"v{h}_loaded") for h in range(2)]
        s_xl = [sem(f"residual{h}_loaded") for h in range(2)]
        s_av = [sem(f"attended_psum{h}") for h in range(2)]
        s_ad = [sem(f"residual{h}_added") for h in range(2)]
        s_out = [sem(f"out{h}_stored") for h in range(2)]

        def when(eng, s, value):
            if not isinstance(value, int) or value > 0:
                eng.wait_ge(s, value)

        NG = C // SI
        SPT = 2 * CI // SI
        REGIONS = [(0, P // (2 * CI), C + E1), (P // (2 * CI), C // (2 * CI), E1)]

        def u_out(eng, pu, k, high):
            for rows, dst_h, dst_l, n, src in (
                    (slice(0, P), UH0, UL0, H, lambda q: q[:, :, 0:C]),
                    (slice(0, E1), UH1, UL1, 2 * H, lambda q: q[:, :, C:2 * C:2]),
                    (slice(E1, P), UH1, UL1, 2 * H, lambda q: q[:, :, C + 1:2 * C:2])):
                off = 4 * k + (H if rows.start else 0)
                s = src(pu[rows]).rearrange("p h i -> p i h")
                dh = dst_h[rows].rearrange("p (i s) -> p i s", s=n)[:, :, off:off + 4]
                dl = dst_l[rows].rearrange("p (i s) -> p i s", s=n)[:, :, off:off + 4]
                if high:
                    ins = eng.activation(dh, s, ACT.Copy, scale=U_SCALE)
                else:
                    ins = eng.scalar_tensor_tensor(dl, s, U_SCALE, dh, ALU.mult, ALU.subtract)
            return ins

        block = ctx.enter_context(nc.Block())

        @block.sync
        def _(sp):
            for c in range(NXC):
                sp.dma_start(X[:, c * XC * E:(c + 1) * XC * E],
                             xs[:, c * XC:(c + 1) * XC, :].rearrange("r c e -> r (c e)")).then_inc(s_x[c], 16)
            for c in range(NCH):
                b = c % 2
                sp.wait_ge(s_l, c + 1)
                dst = xt_dram[c, :, :].rearrange("p (k a n) -> p k a n", k=3, a=2)
                even, mixed, odd = (TT[b][:, t, :, :] for t in range(3))
                sp.dma_start(dst[:, 0:2, 0, :], even).then_inc(s_sp[b], 16)
                sp.dma_start(dst[0:E1, 0:2, 1, :], mixed[E1:P]).then_inc(s_sp[b], 16)
                sp.dma_start(dst[E1:P, 0:2, 1, :], odd[0:E1]).then_inc(s_sp[b], 16)
                for s in range(2):
                    sp.dma_start(dst[s * E1:(s + 1) * E1, 2, 0, :], mixed[0:E1, s, :]).then_inc(s_sp[b], 16)
                    sp.dma_start(dst[s * E1:(s + 1) * E1, 2, 1, :], odd[E1:P, s, :]).then_inc(s_sp[b], 16)
            for b in range(2):
                sp.wait_ge(s_sp[b], STORES * (NCH // 2))
            for h in range(2):
                def load_xt(c, b):
                    sp.dma_start(XT[b], xt_dram[c, :, :]).then_inc(s_xt[h][b], 16)

                def store_v(c, b, second):
                    src = VS[b]
                    if not second:
                        for k in range(2):
                            sp.dma_start(v0_dram[h, bass.ds(c * CI + k * CI // 2, CI // 2), :, :]
                                         .rearrange("i r s -> r i s"),
                                         src[:, k * CI // 2:(k + 1) * CI // 2, :]).then_inc(s_vs[h][b], 16)
                    else:
                        for hl in range(2):
                            sp.dma_start(
                                v1_dram[h, hl, bass.ds(c * CI - P, CI), :, :].rearrange("i r s -> r i s"),
                                src[:, :, hl * EH:(hl + 1) * EH]).then_inc(s_vs[h][b], 16)

                if h == 0:
                    sp.wait_ge(s_sc, NCH)
                    sp.wait_ge(s_sw, 1)
                load_xt(0, 0)
                load_xt(1, 1)

                def chunk(c, b, second):
                    sp.wait_ge(s_pj[h], (c - 1) * CI // SI)
                    load_xt(c, b)
                    sp.wait_ge(s_kvl[h], (c - 1) * CI // SI)
                    store_v(c - 2, b, second)

                with sp.Fori(1, 9) as t:
                    chunk(2 * t, 0, False)
                    chunk(2 * t + 1, 1, False)
                with sp.Fori(9, 12) as t:
                    chunk(2 * t, 0, True)
                    chunk(2 * t + 1, 1, True)
                for b in range(2):
                    sp.wait_ge(s_kvl[h], (NCH - 1 + b) * CI // SI)
                    store_v(NCH - 2 + b, b, True)
                for b in range(2):
                    sp.wait_ge(s_vs[h][b], 32 * (NCH // 2))
                for k in range(HALF):
                    sp.wait_ge(s_qk[h], k + 1)
                    if k < 4:
                        sp.dma_start(V0[:, 32 * k:32 * k + 32, :],
                                     v0_dram[h, :, 32 * k:32 * k + 32, :]).then_inc(s_vl[h], 16)
                    else:
                        r0 = 64 * (k - 4)
                        sp.dma_start(V1[:, r0:r0 + 64, :],
                                     v1_dram[h, :, :, r0:r0 + 64, :].rearrange("s j r e -> (s j) r e")
                                     ).then_inc(s_vl[h], 16)
                    sp.dma_start(XO[:, k * XC:(k + 1) * XC, :],
                                 xs[:, k * XC:(k + 1) * XC, h * EH:(h + 1) * EH]).then_inc(s_xl[h], 16)
                sp.wait_ge(s_ad[h], EH // 4)
                for k in range(2):
                    sp.dma_start(outs[:, k * 96:(k + 1) * 96, h * EH:(h + 1) * EH],
                                 XO[:, k * 96:(k + 1) * 96, :]).then_inc(s_out[h], 16)
            for h in range(2):
                sp.wait_ge(s_out[h], 32)

        @block.gpsimd
        def _(pool):
            pool.memset(ident[:, :], 0.0).then_inc(s_zero, 1)
            pool.memset(ones[:, :], 1.0).then_inc(s_const, 1)
            pool.memset(UH1.bitcast(fp32), 0.0).then_inc(s_const, 1)
            pool.memset(UL1.bitcast(fp32), 0.0).then_inc(s_const, 1)
            pool.memset(res_i[:, :], 1).then_inc(s_zero, 1)
            pool.wait_ge(s_zero, 2)
            pool.affine_select(out=ident[:, :], in_=ident[:, :], compare_op=ALU.not_equal, fill=1.0,
                               base=0, pattern=[[-1, P]], channel_multiplier=1).then_inc(s_const, 1)
            for c in range(NCH):
                b = c % 2
                pool.wait_ge(s_h, c + 1)
                pool.tensor_tensor(TT[b][:, :, 1, :], XN[b], TT[b][:, :, 0, :], ALU.subtract).then_inc(s_l, 1)
            for h in range(2):
                for t0, t1, low in REGIONS:
                    with pool.Fori(t0, t1) as t:
                        for g in range(SPT):
                            n = SPT * t + g
                            pool.wait_ge(s_qh[h], n + 1)
                            pool.tensor_tensor(QA[:, :, bass.ds(SI * n + low, SI)], TQ[g % 4],
                                               QA[:, :, bass.ds(SI * n, SI)],
                                               ALU.subtract).then_inc(s_ql[h], 1)

        @block.scalar
        def _(act):
            act.wait_ge(s_zero, 2)
            for k, w in enumerate((wq, wk, wv, wqs, wks)):
                act.dma_start(W[:, k, 0, :], w[0:P, :]).then_inc(s_params, 16)
                act.dma_start(W[0:E1, k, 1, :], w[P:E, :]).then_inc(s_params, 16)
                act.dma_start(W[E1:P, k, 1, :], w[P:E, :]).then_inc(s_params, 16)
            act.dma_start(X0[:, 0, :], xs[0, 0:P, :]).then_inc(s_params, 16)
            act.dma_start(X0[0:E1, 1, :], xs[0, P:C, :]).then_inc(s_params, 16)
            act.dma_start(seq_i[:, :], seq_mask.rearrange("a r -> r a")).then_inc(s_params, 16)
            act.dma_start(res_i[:, 0:1], res_mask[:, 0:P].rearrange("a r -> r a")).then_inc(s_params, 16)
            act.dma_start(res_i[0:E1, 1:2], res_mask[:, P:C].rearrange("a r -> r a")).then_inc(s_params, 16)
            act.dma_start(row_i, res_mask.partition_broadcast(P).rearrange("p a r -> p (a r)")
                          ).then_inc(s_params, 16)
            act.wait_ge(s_wsc, 1)
            for k in range(3):
                for t in range(2):
                    ins = nc.scalar.copy(WP[:, :, 0, t, k * EH:(k + 1) * EH],
                                         W[:, k, t, :].rearrange("p (a n) -> p a n", a=2))
            ins.then_inc(s_wh, 1)
            act.wait_ge(s_var, 1)
            nc.scalar.activation(t_n, var, ACT.Sqrt).then_inc(s_std, 1)
            act.wait_ge(s_const, 4)
            for k in range(3):
                act.wait_ge(s_u, k + 1)
                pu = PS[:, 4 * (k % 2):4 * (k % 2) + 4, :]
                u_out(nc.scalar, pu, k, True).then_inc(s_uh, 1)
            for c in range(NCH):
                b = c % 2
                act.wait_ge(s_xn, c + 1)
                if c >= 2:
                    act.wait_ge(s_sp[b], STORES * (c // 2))
                    act.wait_ge(s_sc, c - 1)
                nc.scalar.copy(TT[b][:, :, 0, :], XN[b]).then_inc(s_h, 1)
            flat = BIG[:, 0:C * H]
            act.wait_ge(s_ssh, 1)
            nc.scalar.activation(flat, flat, ACT.Exp).then_inc(s_sex, 1)
            act.wait_ge(s_swt, 1)
            nc.scalar.copy(SW[:, :], PS[:, 0:5, :].rearrange("p a b -> p (a b)")[:, 0:C * H]).then_inc(s_sw, 1)

            for h in range(2):
                if h == 1:
                    act.wait_ge(s_out[0], 32)

                def q_high(n, g):
                    act.wait_ge(s_tq[h], n + 1)
                    nc.scalar.copy(QA[:, :, bass.ds(SI * n, SI)], TQ[g % 4]).then_inc(s_qh[h], 1)

                def body(t):
                    for g in range(SPT):
                        n = SPT * t + g
                        ps = PS[:, SI * (g % 4):SI * (g % 4) + SI, 0:3 * EH]
                        at = g % (CI // SI) * SI
                        act.wait_ge(s_pj[h], n + 1)
                        if at == 0:
                            when(act, s_vs[h][g // 4], 32 * t)
                        nc.scalar.copy(VS[g // 4][:, at:at + SI, 0:EH],
                                       ps[:, :, 2 * EH:3 * EH]).then_inc(s_kvh[h], 1)
                        nc.scalar.copy(KA[:, :, bass.ds(SI * n, SI)],
                                       ps[:, :, EH:2 * EH].rearrange("p i m -> p m i")).then_inc(s_kvh[h], 1)
                        if g or not isinstance(t, int):
                            q_high(n - 1, g - 1)

                body(0)
                with act.Fori(1, NG // SPT) as t:
                    body(t)
                q_high(NG - 1, SPT - 1)

                def attention_high(k):
                    act.wait_ge(s_att[h], k + 1)
                    nc.scalar.copy(AT[:, k, 0, :], PS[:, 4 + k % 2, 0:2 * C]).then_inc(s_ath[h], 1)

                for k in range(HALF):
                    act.wait_ge(s_qk[h], k + 1)
                    when(act, s_lr[h], k - 1)
                    nc.scalar.copy(LLOW[k % 2][0:E1, :], PS[E1:P, 2 * (k % 2) + 1, 0:C]).then_inc(s_ll[h], 1)
                    act.wait_ge(s_ls[h], k + 1)
                    nc.scalar.activation(LG[k % 2][:, :, 0:C], LG[k % 2][:, :, 0:C], ACT.Exp).then_inc(s_le[h], 1)
                    if k:
                        attention_high(k - 1)
                attention_high(HALF - 1)

        @block.vector
        def _(dve):
            v = nc.vector
            count = [0]

            def step(ins):
                count[0] += 1
                ins.then_inc(s_dve, 1)
                dve.wait_ge(s_dve, count[0])

            dve.wait_ge(s_const, 4)
            dve.wait_ge(s_params, 16 * N_PARAMS)
            v.tensor_scalar(res01, res_i[:, :], 0, None, ALU.not_equal)
            v.tensor_scalar(seq01, seq_i[:, :], 0, None, ALU.not_equal)
            step(v.tensor_scalar(row01, row_i, 0, None, ALU.not_equal))
            v.tensor_scalar(M01[:, 0, :], row01, res01[:, 0:1], None, ALU.mult)
            step(v.tensor_scalar(seqneg, seq01, -1.0, FMAX, ALU.add, ALU.mult))
            step(v.tensor_scalar(M01[:, 1, :], row01, res01[:, 1:2], None, ALU.mult))
            v.tensor_scalar(NEG[:, :, :], M01[:, :, :], -1.0, FMAX, ALU.add, ALU.mult)
            v.tensor_reduce(parity, ident[:, :].rearrange("p (g a s) -> p a g s", a=2, s=D), AX.XY, ALU.add)
            v.tensor_reduce(mx5, W.rearrange("p w t n -> p w (t n)"), AX.X, ALU.max,
                            apply_absolute_value=True).then_inc(s_wmax, 1)
            dve.wait_ge(s_wmaxT, 1)
            step(v.tensor_reduce(m5t[0:5, :], PS[0:5, 0, 0:P], AX.X, ALU.max))
            v.tensor_scalar(d5[0:5, :], ident[0:5, 0:5], m5t[0:5, :], None, ALU.mult).then_inc(s_wd, 1)
            dve.wait_ge(s_wb, 1)
            step(v.tensor_scalar(mxb, PS[:, 1, 0:5], 1e-30, None, ALU.max))
            step(v.reciprocal(rv5, mxb))
            v.tensor_tensor(W.rearrange("p w t n -> p w (t n)"), W.rearrange("p w t n -> p w (t n)"),
                            rv5.unsqueeze(2).to_broadcast([P, 5, 2 * E]), ALU.mult).then_inc(s_wsc, 1)
            step(v.tensor_tensor(alpha, mxb[:, WQ:WQ + 1], mxb[:, WK:WK + 1], ALU.mult))
            step(v.tensor_scalar(alpha, alpha, 0.17677669529663687 / C ** 0.5 / SW_SCALE, None, ALU.mult))
            step(v.tensor_tensor(seqscale, mxb[:, WQS:WQS + 1], mxb[:, WKS:WKS + 1], ALU.mult))
            step(v.tensor_scalar(seqscale, seqscale, seq01, 1.0 / D ** 0.5 / U_SCALE, ALU.mult, ALU.mult))
            dve.wait_ge(s_wkt, 1)
            v.tensor_copy(WKT[:, 0, :], PS[:, 2, 0:256])
            step(v.tensor_copy(WKT[0:E1, 1, :], PS[0:E1, 2, 256:512]))
            dve.wait_ge(s_wh, 1)
            for k in range(3):
                for t in range(2):
                    v.tensor_tensor(WP[:, :, 1, t, k * EH:(k + 1) * EH],
                                    W[:, k, t, :].rearrange("p (a n) -> p a n", a=2),
                                    WP[:, :, 0, t, k * EH:(k + 1) * EH], ALU.subtract)
            for c in range(NXC):
                dve.wait_ge(s_x[c], 16)
                xv = X[:, c * XC * E:(c + 1) * XC * E].rearrange("p (i e) -> p i e", e=E)
                for g in range(G):
                    ins = v.bn_stats(ST[:, g, c, :], xv[:, :, g * GC:(g + 1) * GC])
            step(ins)
            sv = ST.rearrange("p g c (a s) -> p g (c a) s", s=3)
            K = 2 * NXC
            n_sub = XC * GC // 2
            v.tensor_reduce(s1, sv[:, :, :, 1], AX.X, ALU.add).then_inc(s_st1, 1)
            step(v.tensor_reduce(s3, sv[:, :, :, 2], AX.X, ALU.add))
            dve.wait_ge(s_mm1, 1)
            step(v.tensor_scalar(mean, PS[:, 1, 0:G], 1.0 / (K * R), None, ALU.mult))
            step(v.tensor_tensor(DM, sv[:, :, :, 1], mean.unsqueeze(2).to_broadcast([P, G, K]), ALU.subtract))
            step(v.tensor_tensor(DM, DM, DM, ALU.mult))
            step(v.tensor_reduce(s2, DM, AX.X, ALU.add))
            v.scalar_tensor_tensor(s2, s2, float(n_sub), s3, ALU.mult, ALU.add).then_inc(s_st2, 1)
            dve.wait_ge(s_mm2, 1)
            v.tensor_scalar(var, PS[:, 0, 0:G], 1.0 / (n_sub * K * R), EPS, ALU.mult,
                            ALU.add).then_inc(s_var, 1)
            dve.wait_ge(s_std, 1)
            step(v.reciprocal(y, t_n))
            step(v.tensor_tensor(t_n, y, y, ALU.mult))
            step(v.tensor_tensor(t_n, t_n, var, ALU.mult))
            step(v.tensor_scalar(t_n, t_n, -0.5, 1.5, ALU.mult, ALU.add))
            step(v.tensor_tensor(y, y, t_n, ALU.mult))
            step(v.scalar_tensor_tensor(y2, mean, -1.0, y, ALU.mult, ALU.mult))
            for k, q in enumerate((y, y2)):
                step(v.tensor_copy(AB[:, k, 0:E].rearrange("p (g s) -> p g s", s=GC),
                                   q.unsqueeze(2).to_broadcast([P, G, GC])))
            v.tensor_copy(AB[:, :, E:256], AB[:, :, 0:E1]).then_inc(s_ab, 1)
            dve.wait_ge(s_abT, 1)
            step(v.tensor_copy(abc, PS[:, 1, 0:6]))
            v.tensor_scalar(QX[:, 0, :], PS[:, 3, 0:C], abc[:, 0:1], abc[:, 3:4], ALU.mult, ALU.add)
            v.tensor_scalar(QX[0:E1, 1, :], PS[0:E1, 3, C:2 * C], abc[0:E1, 1:2], abc[0:E1, 4:5],
                            ALU.mult, ALU.add).then_inc(s_x0n, 1)
            dve.wait_ge(s_qs, 1)
            for a in range(2):
                v.tensor_scalar(QM[:, 0, a, :], PS[:, 0, 0:C], parity[:, a:a + 1], None, ALU.mult)
            for a in range(2):
                ins = v.tensor_scalar(QM[0:E1, 1, a, :], PS[0:E1, 0, C:2 * C], parity[0:E1, a:a + 1], None,
                                      ALU.mult)
            ins.then_inc(s_qm, 1)
            for k in range(3):
                dve.wait_ge(s_uh, k + 1)
                u_out(v, PS[:, 4 * (k % 2):4 * (k % 2) + 4, :], k, False).then_inc(s_ul, 1)

            def score(c):
                dve.wait_ge(s_sc, c + 1)
                v.tensor_scalar(SW[:, c * CI * H:(c + 1) * CI * H], PS[:, 6 + c % 2, 0:CI * H],
                                seqscale, seqneg, ALU.mult, ALU.add).then_inc(s_se, 1)

            for c in range(NCH):
                b = c % 2
                dve.wait_ge(s_tr, c + 1)
                when(dve, s_l, c - 1)
                for k in range(3):
                    ins = v.tensor_scalar(XN[b][:, k, :], PS[:, 3 * b + k, :], abc[:, k:k + 1],
                                          abc[:, 3 + k:4 + k], ALU.mult, ALU.add)
                ins.then_inc(s_xn, 1)
                if c >= 2:
                    score(c - 2)
            score(NCH - 2)
            score(NCH - 1)
            flat = BIG[:, 0:C * H].rearrange("p (k r) -> p k r", r=R)
            st = PS[:, 0:5, :].rearrange("p a b -> p (a b)")[:, 0:C * H].rearrange("p (k r) -> p k r", r=R)
            dve.wait_ge(s_stt, 1)
            step(v.tensor_reduce(smx, st, AX.X, ALU.max))
            v.tensor_tensor(flat, st, smx.unsqueeze(2).to_broadcast([P, 18, R]), ALU.subtract).then_inc(s_ssh, 1)
            dve.wait_ge(s_sex, 1)
            step(v.tensor_reduce(ssum, flat, AX.X, ALU.add))
            step(v.reciprocal(sinv, ssum))
            step(v.tensor_scalar(sinv, sinv, SW_SCALE, None, ALU.mult))
            v.tensor_tensor(flat, flat, sinv.unsqueeze(2).to_broadcast([P, 18, R]), ALU.mult).then_inc(s_snm, 1)
            dve.wait_ge(s_sw, 1)

            for h in range(2):
                def body(t):
                    for g in range(SPT):
                        n = SPT * t + g
                        ps = PS[:, SI * (g % 4):SI * (g % 4) + SI, 0:3 * EH]
                        at = g % (CI // SI) * SI
                        dve.wait_ge(s_kvh[h], 2 * n + 2)
                        when(dve, s_ql[h], n - 3)
                        swv = SW[:, bass.ds(SI * n * H, SI * H)].rearrange("p (i m) -> p m i", m=H)
                        swv = swv[:, h * HALF:(h + 1) * HALF, :]
                        v.tensor_tensor(TQ[g % 4].rearrange("p (m d) i -> p m d i", d=D),
                                        ps[:, :, 0:EH].rearrange("p i (m d) -> p m d i", d=D),
                                        swv.unsqueeze(2).to_broadcast([P, HALF, D, SI]),
                                        ALU.mult).then_inc(s_tq[h], 1)
                        vs = VS[g // 4][:, at:at + SI, :]
                        v.tensor_tensor(vs[:, :, EH:2 * EH], ps[:, :, 2 * EH:3 * EH], vs[:, :, 0:EH],
                                        ALU.subtract)
                        v.tensor_tensor(KA[:, :, bass.ds(SI * n + C, SI)],
                                        ps[:, :, EH:2 * EH].rearrange("p i m -> p m i"),
                                        KA[:, :, bass.ds(SI * n, SI)], ALU.subtract).then_inc(s_kvl[h], 1)

                body(0)
                with dve.Fori(1, NG // SPT) as t:
                    body(t)

                if h == 0:
                    for b in range(2):
                        v.memset(LG[b][E1:P, 1, :], 0.0)

                def attention_low(k):
                    dve.wait_ge(s_ath[h], k + 1)
                    v.tensor_tensor(AT[:, k, 1, :], PS[:, 4 + k % 2, 0:2 * C], AT[:, k, 0, :],
                                    ALU.subtract).then_inc(s_atl[h], 1)

                for k in range(HALF):
                    lg = LG[k % 2]
                    lv = lg[:, :, 0:C]
                    dve.wait_ge(s_qk[h], k + 1)
                    when(dve, s_att[h], k - 1)
                    v.scalar_tensor_tensor(lg[:, 0, 0:C], PS[:, 2 * (k % 2), 0:C], alpha, M01[:, 0, :],
                                           ALU.mult, ALU.mult)
                    dve.wait_ge(s_ll[h], k + 1)
                    ins = v.tensor_tensor(lg[0:E1, 1, 0:C], PS[0:E1, 2 * (k % 2) + 1, 0:C],
                                          LLOW[k % 2][0:E1, :], ALU.add)
                    ins.then_inc(s_lr[h], 1)
                    dve.wait_ge(s_lr[h], k + 1)
                    step(v.scalar_tensor_tensor(lg[0:E1, 1, 0:C], lg[0:E1, 1, 0:C], alpha[0:E1, :],
                                                M01[0:E1, 1, :], ALU.mult, ALU.mult))
                    step(v.tensor_tensor(lv, lv, NEG[:, :, :], ALU.add))
                    step(v.tensor_reduce(lmx, lv, AX.X, ALU.max))
                    v.tensor_tensor(lv, lv, lmx.unsqueeze(2).to_broadcast([P, 2, C]),
                                    ALU.subtract).then_inc(s_ls[h], 1)
                    dve.wait_ge(s_le[h], k + 1)
                    step(v.tensor_reduce(lsum, lv, AX.X, ALU.add))
                    step(v.reciprocal(linv, lsum))
                    step(v.tensor_tensor(lg[:, :, C:256], lg[:, :, P:C],
                                         linv.unsqueeze(2).to_broadcast([P, 2, E1]), ALU.mult))
                    v.tensor_tensor(lv, lv, linv.unsqueeze(2).to_broadcast([P, 2, C]),
                                    ALU.mult).then_inc(s_at[h], 1)
                    if k:
                        attention_low(k - 1)
                attention_low(HALF - 1)

                dve.wait_ge(s_xl[h], 16 * NXC)
                for m in range(EH // 4):
                    b = m % 4
                    dve.wait_ge(s_av[h], m + 1)
                    o = XO[:, :, 4 * m:4 * m + 4]
                    got = PS[:, 2 * b:2 * b + 2, :].rearrange("p a (b i) -> p i (a b)", b=2)[:, 0:C, :]
                    v.scalar_tensor_tensor(
                        o, got, mxb[:, WV:WV + 1], o, ALU.mult, ALU.add).then_inc(s_ad[h], 1)

        @block.tensor
        def _(pe):
            mm = nc.tensor.matmul
            pe.wait_ge(s_const, 4)
            pe.wait_ge(s_wmax, 1)
            nc.tensor.transpose(PS[0:5, 0, 0:P], mx5, ident[:, :]).then_inc(s_wmaxT, 1)
            pe.wait_ge(s_wd, 1)
            mm(PS[:, 1, 0:5], ones[0:5, :], d5[0:5, :], start=True, stop=True).then_inc(s_wb, 1)
            pe.wait_ge(s_wsc, 1)
            nc.tensor.transpose(PS[:, 2, 0:P], W[:, WKS, 0, 0:P], ident[:, :])
            nc.tensor.transpose(PS[:, 2, P:E], W[0:E1, WKS, 1, 0:P], ident[0:E1, 0:E1])
            nc.tensor.transpose(PS[:, 2, E:256], W[0:E1, WKS, 0, 0:P], ident[0:E1, 0:E1])
            nc.tensor.transpose(PS[0:E1, 2, 256:384], W[:, WKS, 0, P:E], ident[:, :])
            nc.tensor.transpose(PS[0:E1, 2, 384:448], W[0:E1, WKS, 1, P:E], ident[0:E1, 0:E1])
            nc.tensor.transpose(PS[0:E1, 2, 448:512], W[0:E1, WKS, 0, P:E], ident[0:E1, 0:E1])
            nc.tensor.transpose(PS[:, 3, 0:P], X0[:, 0, 0:P], ident[:, :])
            nc.tensor.transpose(PS[:, 3, P:C], X0[0:E1, 1, 0:P], ident[0:E1, 0:E1])
            nc.tensor.transpose(PS[0:E1, 3, C:C + P], X0[:, 0, P:E], ident[:, :])
            nc.tensor.transpose(PS[0:E1, 3, C + P:2 * C], X0[0:E1, 1, P:E], ident[0:E1, 0:E1]).then_inc(s_wkt, 1)
            pe.wait_ge(s_st1, 1)
            mm(PS[:, 1, 0:G], ones[:, :], s1, start=True, stop=True).then_inc(s_mm1, 1)
            pe.wait_ge(s_st2, 1)
            mm(PS[:, 0, 0:G], ones[:, :], s2, start=True, stop=True).then_inc(s_mm2, 1)
            pe.wait_ge(s_ab, 1)
            for k in range(2):
                for t, e0 in enumerate((0, P, E1)):
                    ins = mm(PS[:, 1, 3 * k + t:3 * k + t + 1], AB[0:1, k, e0:e0 + P],
                             ones[0:1, 0:1], start=True, stop=True)
            ins.then_inc(s_abT, 1)
            pe.wait_ge(s_x0n, 1)
            for m, (lo, n) in enumerate(((0, P), (P, E1))):
                po = PS[0:n, 0, m * C:(m + 1) * C]
                mm(po, W[:, WQS, 0, lo:lo + n], QX[:, 0, :], start=True, stop=False)
                ins = mm(po, W[0:E1, WQS, 1, lo:lo + n], QX[0:E1, 1, :], start=False, stop=True)
            ins.then_inc(s_qs, 1)
            pe.wait_ge(s_qm, 1)
            for hd in range(H):
                t, row, par, k = hd // 8, 32 * ((hd % 8) // 2), hd % 2, hd // 4
                if hd % 4 == 0 and k >= 2:
                    pe.wait_ge(s_ul, k - 1)
                bank = 4 * (k % 2) + hd % 4
                for o, n, e0, cols in ((0, C // 2, 0, QM[row:row + 32, t, par, 0:C:2]),
                                       (C // 2, C // 2, E1, QM[row:row + 32, t, par, 1:C:2]),
                                       (C, C, P, QM[row:row + 32, t, par, :])):
                    ins = mm(PS[:, bank, o:o + n], WKT[row:row + 32, t, e0:e0 + P], cols, start=True, stop=True)
                if hd % 4 == 3:
                    ins.then_inc(s_u, 1)
            pe.wait_ge(s_ul, 3)

            def scores(c):
                b = c % 2
                pe.wait_ge(s_l, c + 1)
                pe.wait_ge(s_h, c + 1)
                when(pe, s_se, c - 1)
                first = True
                for q in range(CI // 2):
                    j = c * CI // 2 + q
                    for a in range(2):
                        for s, u in ((0, UH0), (0, UL0), (1, UH0)):
                            mm(PS[:, 6 + b, (2 * q + a) * H:(2 * q + a + 1) * H],
                               TT[b][:, 2 * a, s, q * P:(q + 1) * P],
                               u[:, (a * C // 2 + j) * H:(a * C // 2 + j + 1) * H],
                               start=first, stop=False, skip_group_check=True)
                            first = False
                    for s, u in ((0, UH1), (0, UL1), (1, UH1)):
                        ins = mm(PS[:, 6 + b, 2 * q * H:(2 * q + 2) * H], TT[b][:, 1, s, q * P:(q + 1) * P],
                                 u[:, j * 2 * H:(j + 1) * 2 * H], start=False, stop=True,
                                 skip_group_check=True)
                ins.then_inc(s_sc, 1)

            for c in range(NCH):
                b = c % 2
                when(pe, s_xn, c - 1)
                for q in range(CI // 2):
                    for k in range(3):
                        at = (c * CI + 2 * q) * E + k * P
                        ins = nc.tensor.transpose(PS[:, 3 * b + k, q * P:(q + 1) * P], X[:, at:at + P],
                                                  ident[:, :])
                ins.then_inc(s_tr, 1)
                if c:
                    scores(c - 1)
            scores(NCH - 1)
            pe.wait_ge(s_se, NCH)
            for k in range(18):
                ins = nc.tensor.transpose(PS[:, k // 4, (k % 4) * P:(k % 4 + 1) * P],
                                          SW[:, k * P:(k + 1) * P], ident[:, :])
            ins.then_inc(s_stt, 1)
            pe.wait_ge(s_snm, 1)
            for k in range(18):
                ins = nc.tensor.transpose(PS[:, k // 4, (k % 4) * P:(k % 4 + 1) * P],
                                          BIG[:, k * P:(k + 1) * P], ident[:, :])
            ins.then_inc(s_swt, 1)
            pe.wait_ge(s_sw, 1)

            for h in range(2):
                def body(t):
                    for g in range(SPT):
                        n = SPT * t + g
                        b = g // 4
                        if g % 4 == 0:
                            pe.wait_ge(s_xt[h][b], 16 * (t + 1))
                        when(pe, s_kvl[h], n - 3)
                        for i in range(SI):
                            il = SI * (g % 4) + i
                            po = PS[:, il, 0:3 * EH]
                            slot = (il % 2) * (CI // 2) + il // 2
                            xh0 = XT[b][:, slot * R:(slot + 1) * R]
                            xl0 = XT[b][:, (CI + slot) * R:(CI + slot + 1) * R]
                            x1 = XT[b][:, (2 * CI + slot) * R:(2 * CI + slot + 1) * R]
                            mm(po, xh0, WP[:, h, 0, 0, :], start=True, stop=False)
                            mm(po, xh0, WP[:, h, 1, 0, :], start=False, stop=False)
                            mm(po, xl0, WP[:, h, 0, 0, :], start=False, stop=False)
                            mm(po, x1, WP[:, h, 0, 1, :], start=False, stop=False)
                            ins = mm(po, x1, WP[:, h, 1, 1, :], start=False, stop=True)
                        ins.then_inc(s_pj[h], 1)

                body(0)
                with pe.Fori(1, NG // SPT) as t:
                    body(t)

                def transposes(k):
                    lg = LG[k % 2]
                    pe.wait_ge(s_at[h], k + 1)
                    when(pe, s_atl[h], k - 1)
                    pb = PS[:, 4 + k % 2, :]
                    nc.tensor.transpose(pb[:, 0:P], lg[:, 0, 0:P], ident[:, :])
                    nc.tensor.transpose(pb[:, P:C], lg[0:E1, 1, 0:P], ident[0:E1, 0:E1])
                    nc.tensor.transpose(pb[:, C:C + P], lg[:, 0, P:256], ident[:, :])
                    nc.tensor.transpose(pb[:, C + P:2 * C], lg[0:E1, 1, P:256],
                                        ident[0:E1, 0:E1]).then_inc(s_att[h], 1)

                pe.wait_ge(s_ql[h], NG)
                pe.wait_ge(s_kvl[h], NG)
                for k in range(HALF):
                    when(pe, s_lr[h], k - 1)
                    for d in range(D):
                        m = k * D + d
                        first, last = d == 0, d == D - 1
                        p0, p1 = PS[:, 2 * (k % 2), 0:C], PS[:, 2 * (k % 2) + 1, 0:C]
                        kh, kl = KA[:, m, 0:C], KA[:, m, C:2 * C]
                        mm(p0, QA[:, m, 0:P], kh, start=first, stop=False)
                        mm(p0, QA[:, m, 0:P], kl, start=False, stop=False)
                        mm(p0, QA[:, m, 2 * P:3 * P], kh, start=False, stop=last)
                        mm(p1, QA[:, m, P:2 * P], kh, start=first, stop=False)
                        ins = mm(p1, QA[:, m, P:2 * P], kl, start=False, stop=last)
                    ins.then_inc(s_qk[h], 1)
                    if k:
                        transposes(k - 1)
                transposes(HALF - 1)

                pe.wait_ge(s_vl[h], 16 * HALF)
                pe.wait_ge(s_atl[h], HALF)
                for m in range(EH // 4):
                    b = m % 4
                    when(pe, s_ad[h], m - 3)
                    for j in range(4):
                        e = 4 * m + j
                        k = e // D
                        po = PS[:, 2 * b + j // 2, (j % 2) * 256:(j % 2) * 256 + C]
                        a0h, a1h = AT[:, k, 0, 0:C], AT[:, k, 0, C:2 * C]
                        a0l, a1l = AT[:, k, 1, 0:C], AT[:, k, 1, C:2 * C]
                        mm(po, V0[:, :, e], a0h, start=True, stop=False)
                        mm(po, V0[:, :, e], a0l, start=False, stop=False)
                        mm(po, V0[:, :, EH + e], a0h, start=False, stop=False)
                        mm(po, V1[:, :, e], a1h, start=False, stop=False)
                        ins = mm(po, V1[:, :, e], a1l, start=False, stop=True)
                    ins.then_inc(s_av[h], 1)
                pe.wait_ge(s_ad[h], EH // 4)


_INS = ["x", "L0_conv_Wq", "L0_conv_Wk", "L0_conv_Wv", "L0_conv_Wq_s", "L0_conv_Wk_s",
        "L0_conv_res_mask", "L0_conv_seq_mask"]


def kernel(**inputs):
    import numpy as _np
    import concourse.bacc as _bacc
    from concourse import mybir as _mybir
    from concourse.bass_utils import run_bass_kernel_spmd as _run

    nc = _bacc.Bacc("TRN2", target_bir_lowering=False, num_devices=1)
    arrays, args = {}, []
    for name in _INS:
        a = _np.ascontiguousarray(inputs[name])
        arrays[f"in_{name}"] = a
        args.append(nc.dram_tensor(f"in_{name}", a.shape, _mybir.dt.from_np(a.dtype), kind="ExternalInput").ap())
    args.append(nc.dram_tensor("out_x", (1, R, C, E), _mybir.dt.float32, kind="ExternalOutput").ap())
    row_column_attention(nc, *args)
    r = _run(nc, [arrays], core_ids=[0])
    return r.results[0]["out_x"]
```

```python
import concourse.bass as bass
from concourse import mybir
from contextlib import ExitStack

fp32 = mybir.dt.float32
fp16 = mybir.dt.float16
int32 = mybir.dt.int32
ALU = mybir.AluOpType
ACT = mybir.ActivationFunctionType
AX = mybir.AxisListType

R, C, E, H = 128, 192, 192, 12
D = E // H
G, GC = 32, E // 32
P = 128
E1 = E - P
HALF = H // 2
EH = HALF * D
FMAX = 3.4028234663852886e38
EPS = 1e-5
U_SCALE = 0.125
SW_SCALE = 2.0
CI = 8
SI = (2, 4)
CW = (2 * EH + E, 2 * EH)
RI = 16
NRC = R // RI
NCH = C // CI
XC = 32
NXC = C // XC
WQ, WK, WV, WQS, WKS = range(5)


def row_column_attention(nc, x, wq, wk, wv, wqs, wks, res_mask, seq_mask, out):
    xs = x.rearrange("b r c e -> (b r) c e")
    outs = out.rearrange("b r c e -> (b r) c e")

    xt_dram = nc.dram_tensor("xt_scratch", [NCH // 2, P, 6 * CI * R], fp16, kind="Internal").ap()
    v0_dram = nc.dram_tensor("v0_scratch", [P, R, 2 * E], fp16, kind="Internal").ap()
    v1_dram = nc.dram_tensor("v1_scratch", [2, E1, R, E], fp16, kind="Internal").ap()

    ctx = ExitStack()
    with ctx:
        def sb(name, shape, dt=fp32):
            return ctx.enter_context(nc.sbuf_tensor(name, shape, dt))

        def sem(name):
            return ctx.enter_context(nc.semaphore(name))

        BIG = sb("BIG", [P, C * E])
        X = BIG[:, :]
        AR = C * E // 2
        QA = BIG[:, 0:AR].bitcast(fp16).rearrange("p (m s) -> p m s", s=2 * C)
        KA = BIG[:, AR:2 * AR].bitcast(fp16).rearrange("p (m s) -> p m s", s=2 * C)
        TT = [BIG[:, c * CI * E:(c + 1) * CI * E].bitcast(fp16).rearrange("p (s t n) -> p t s n", t=3, s=2)
              for c in range(NCH)]
        VN = 3 * RI * E // 2
        V0 = [BIG[:, k * VN:k * VN + RI * E].bitcast(fp16).rearrange("p (r s e) -> p r s e", s=2, e=E)
              for k in range(4)]
        V1 = [BIG[:, k * VN + RI * E:(k + 1) * VN].bitcast(fp16).rearrange("p (r e) -> p r e", e=E)
              for k in range(4)]
        XO = [BIG[:, AR + 2 * k * RI * E:AR + 2 * (k + 1) * RI * E].rearrange("p (t r e) -> p t r e", t=2, e=E)
              for k in range(3)]

        EXTRA = sb("EXTRA", [P, 10496])
        place = [0]

        def part(n):
            place[0] += n
            return EXTRA[:, place[0] - n:place[0]]

        UH0, UL0, UH1, UL1 = (part(C * H // 2).bitcast(fp16) for _ in range(4))
        after_u = place[0]
        XN = [part(CI * E).rearrange("p (t n) -> p t n", t=3) for _ in range(3)]
        place[0] = after_u
        W = part(5 * 2 * E).rearrange("p (w t n) -> p w t n", w=5, t=2)
        ST = part(G * NXC * 6).rearrange("p (g c s) -> p g c s", g=G, c=NXC)
        WKT = part(2 * 256).rearrange("p (t n) -> p t n", t=2)
        QM = part(4 * C).rearrange("p (t a n) -> p t a n", t=2, a=2)
        X0 = part(2 * E).rearrange("p (t n) -> p t n", t=2)
        QX = part(2 * C).rearrange("p (t n) -> p t n", t=2)
        AB = part(2 * 256).rearrange("p (t n) -> p t n", t=2)
        row_i = part(C).bitcast(int32)
        place[0] = 0
        XT = [part(3 * CI * R // 2).bitcast(fp16) for _ in range(2)]
        at_first = place[0]
        VS = [part(CI * E).bitcast(fp16).rearrange("p (i s) -> p i s", s=2 * E) for _ in range(2)]
        at_tq = place[0]
        TQ = [[part(4 * EH) for _ in range(4)]]
        TQ = [[q[:, 0:SI[h] * EH].rearrange("p (m i) -> p m i", i=SI[h]) for q in TQ[0]] for h in range(2)]
        FLAT = part(C * H)
        AT = [EXTRA[:, o:o + HALF * 2 * C].bitcast(fp16).rearrange("p (h t n) -> p h t n", h=HALF, t=2)
              for o in (at_first, 0)]
        place[0] = at_tq
        LG = [part(2 * 256).rearrange("p (t n) -> p t n", t=2) for _ in range(2)]
        LLOW = [part(C) for _ in range(2)]
        OLOW = [EXTRA[:, at_tq + k * 512:at_tq + (k + 1) * 512] for k in range(3)]

        SW = sb("SW", [P, C * H])
        DM = SW[:, 0:G * 2 * NXC].rearrange("p (g k) -> p g k", g=G)
        WP = sb("WP", [P, 2, 2, sum(CW)], fp16)
        ident = sb("ident", [P, P])
        ones = sb("ones", [P, P])
        M01 = sb("M01", [P, 2, C])
        NEG = sb("NEG", [P, 2, C])
        small = sb("small", [P, 512])
        sp = [0]

        def col(n):
            sp[0] += n
            return small[:, sp[0] - n:sp[0]]

        seq_i = sb("seq_i", [P, 1], int32)
        res_i = sb("res_i", [P, 2], int32)
        seq01, seqneg, seqscale = col(1), col(1), col(1)
        res01 = col(2)
        parity = col(2)
        mx5, m5t, mxb, rv5, d5 = col(5), col(1), col(5), col(5), col(5)
        alpha = col(1)
        s1, mean, s2, s3, var, y, t_n, y2 = (col(G) for _ in range(8))
        abc = col(6)
        smx, ssum, sinv = col(18), col(18), col(18)
        lmx, lsum, linv = col(2), col(2), col(2)
        row01 = M01[:, 1, :]

        PS = ctx.enter_context(nc.psum_tensor("PS", [P, 8, 512], fp32))

        s_x = [sem(f"x_loaded{c}") for c in range(NXC)]
        s_params = sem("params_loaded")
        STORES = 16 * 7
        N_PARAMS = 5 * 3 + 2 + 4
        s_zero = sem("tiles_zeroed")
        s_const = sem("constants_ready")
        s_dve = sem("vector_step")
        s_wmax = sem("weight_max_ready")
        s_wmaxT = sem("weight_max_transposed")
        s_wd = sem("weight_max_diagonal")
        s_wb = sem("weight_max_everywhere")
        s_wsc = sem("weights_scaled")
        s_wh = sem("weight_highs_ready")
        s_wl = sem("weight_lows_ready")
        s_wkt = sem("wks_and_x0_transposed")
        s_st1 = sem("row_means_summed")
        s_mm1 = sem("means_added")
        s_st2 = sem("squares_summed")
        s_mm2 = sem("squares_added")
        s_var = sem("variance_ready")
        s_std = sem("deviation_ready")
        s_ab = sem("scale_shift_rows")
        s_abT = sem("scale_shift_columns_psum")
        s_x0n = sem("x0_normalised")
        s_qs = sem("row_queries_psum")
        s_qm = sem("row_queries_masked")
        s_u = sem("score_vectors_psum")
        s_uh = sem("score_vector_highs")
        s_ul = sem("score_vectors_split")
        s_tr = sem("x_transposed")
        s_xn = sem("xnT_ready")
        s_h = sem("xnT_highs")
        s_l = sem("xnT_lows")
        s_sp = sem("xnT_stored")
        s_xc = sem("xnT_odd_tile_ready")
        s_ld = sem("xnT_even_tile_lows")
        s_sc = sem("scores_psum")
        s_se = sem("scores_ready")
        s_stt = sem("scores_transposed")
        s_ssh = sem("scores_shifted")
        s_sex = sem("scores_exponent")
        s_snm = sem("row_weights_normalised")
        s_swt = sem("row_weights_psum")
        s_sw = sem("row_weights_ready")
        s_xt = [[sem(f"xt{h}_loaded{b}") for b in range(2)] for h in range(2)]
        s_pj = [sem(f"projected{h}") for h in range(2)]
        s_kvh = [sem(f"kv_highs{h}") for h in range(2)]
        s_kvl = [sem(f"kv_lows{h}") for h in range(2)]
        s_tq = [sem(f"weighted_q{h}") for h in range(2)]
        s_qh = [sem(f"q_highs{h}") for h in range(2)]
        s_ql = [sem(f"q_lows{h}") for h in range(2)]
        s_vs = [sem(f"v_stored{b}") for b in range(2)]
        s_qk = [sem(f"logits_psum{h}") for h in range(2)]
        s_ll = [sem(f"logits_low_part{h}") for h in range(2)]
        s_lr = [sem(f"logits_read{h}") for h in range(2)]
        s_ls = [sem(f"logits_shifted{h}") for h in range(2)]
        s_le = [sem(f"logits_exponent{h}") for h in range(2)]
        s_at = [sem(f"attention_ready{h}") for h in range(2)]
        s_att = [sem(f"attention_transposed{h}") for h in range(2)]
        s_ath = [sem(f"attention_highs{h}") for h in range(2)]
        s_atl = [sem(f"attention_lows{h}") for h in range(2)]
        s_vl = [sem(f"v_loaded{k}") for k in range(4)]
        s_xl = [sem(f"residual_loaded{k}") for k in range(3)]
        s_av = sem("attended_psum")
        s_ad = sem("residual_added")
        s_ol = sem("attended_low_part")
        s_lo = sem("low_part_added")
        s_out = [sem(f"out_stored{k}") for k in range(3)]

        def when(eng, s, value):
            if not isinstance(value, int) or value > 0:
                eng.wait_ge(s, value)

        NG = [C // n for n in SI]
        SPT = [2 * CI // n for n in SI]

        def projected(h, g):
            ps = PS[:, 2 * (g % 4):2 * (g % 4) + 2, :]
            return ps if h == 0 else ps.rearrange("p a (b n) -> p (a b) n", b=2)

        REGIONS = [(0, P // (2 * CI), C + E1), (P // (2 * CI), C // (2 * CI), E1)]

        def u_out(eng, pu, k, high):
            for rows, dst_h, dst_l, n, src in (
                    (slice(0, P), UH0, UL0, H, lambda q: q[:, :, 0:C]),
                    (slice(0, E1), UH1, UL1, 2 * H, lambda q: q[:, :, C:2 * C:2]),
                    (slice(E1, P), UH1, UL1, 2 * H, lambda q: q[:, :, C + 1:2 * C:2])):
                off = 4 * k + (H if rows.start else 0)
                s = src(pu[rows]).rearrange("p h i -> p i h")
                dh = dst_h[rows].rearrange("p (i s) -> p i s", s=n)[:, :, off:off + 4]
                dl = dst_l[rows].rearrange("p (i s) -> p i s", s=n)[:, :, off:off + 4]
                if high:
                    ins = eng.activation(dh, s, ACT.Copy, scale=U_SCALE)
                else:
                    ins = eng.scalar_tensor_tensor(dl, s, U_SCALE, dh, ALU.mult, ALU.subtract)
            return ins

        W_PARTS = ((0, WQ, 0, EH), (EH, WK, 0, EH), (2 * EH, WV, 0, E),
                   (CW[0], WQ, EH, EH), (CW[0] + EH, WK, EH, EH))
        placed = {"load_v": 0, "load_x": 0}
        BPC = H

        block = ctx.enter_context(nc.Block())

        @block.sync
        def _(sp):
            for c in range(NXC):
                if c == 1:
                    sp.wait_ge(s_params, 16 * N_PARAMS)
                sp.dma_start(X[:, c * XC * E:(c + 1) * XC * E],
                             xs[:, c * XC:(c + 1) * XC, :].rearrange("r c e -> r (c e)")).then_inc(s_x[c], 16)
            for c in range(0, NCH, 2):
                sp.wait_ge(s_l, c + 2)
                sp.wait_ge(s_ld, c + 2)
                full = xt_dram[c // 2, :, 0:4 * CI * R].rearrange("p (c a n) -> p c a n", a=2, n=512)
                rest = xt_dram[c // 2, :, 4 * CI * R:6 * CI * R].rearrange("p (c a n) -> p c a n", a=2, n=512)
                src = BIG[:, c * CI * E:(c + 2) * CI * E].bitcast(fp16)
                src = src.rearrange("p (c t n) -> p c t n", t=3, n=512)
                even, mixed, odd = (src[:, :, t, :] for t in range(3))
                sp.dma_start(full[:, :, 0, :], even).then_inc(s_sp, 16)
                sp.dma_start(full[0:E1, :, 1, :], mixed[E1:P]).then_inc(s_sp, 16)
                sp.dma_start(full[E1:P, :, 1, :], odd[0:E1]).then_inc(s_sp, 16)
                for s in range(2):
                    to = rest[s * E1:(s + 1) * E1]
                    sp.dma_start(to[:, :, 0, :], mixed[0:E1, s::2, :]).then_inc(s_sp, 16)
                    sp.dma_start(to[:, :, 1, :], odd[E1:P, s::2, :]).then_inc(s_sp, 16)
            sp.wait_ge(s_sc, NCH)
            sp.wait_ge(s_sp, STORES * NCH // 2)
            for h in range(2):
                def load_xt(t, b):
                    pair = xt_dram[bass.ds(t, 1), :, :].rearrange("a p n -> p (a n)")
                    n0, n1 = 2 * CI * R, 4 * CI * R
                    sp.dma_start(XT[b][:, 0:n0], pair[:, b * n0:(b + 1) * n0]).then_inc(s_xt[h][b], 16)
                    sp.dma_start(XT[b][:, n0:], pair[:, n1 + b * CI * R:n1 + (b + 1) * CI * R]
                                 ).then_inc(s_xt[h][b], 16)

                def store_v(c, b, second):
                    for k in range(2):
                        if not second:
                            cols = slice(k * CI // 2, (k + 1) * CI // 2)
                            sp.dma_start(v0_dram[bass.ds(c * CI + k * CI // 2, CI // 2), :, :]
                                         .rearrange("i r s -> r i s"), VS[b][:, cols, :]).then_inc(s_vs[b], 16)
                        else:
                            sp.dma_start(v1_dram[k, bass.ds(c * CI - P, CI), :, :].rearrange("i r s -> r i s"),
                                         VS[b][:, :, k * E:(k + 1) * E]).then_inc(s_vs[b], 16)

                load_xt(0, 0)
                load_xt(0, 1)

                def chunk(t, b, second):
                    c = 2 * t + b
                    sp.wait_ge(s_pj[h], (c - 1) * (CI // SI[h]))
                    load_xt(t, b)
                    if h == 0:
                        sp.wait_ge(s_kvl[h], (c - 1) * (CI // SI[h]))
                        store_v(c - 2, b, second)

                with sp.Fori(1, 9) as t:
                    chunk(t, 0, False)
                    chunk(t, 1, False)
                with sp.Fori(9, 12) as t:
                    chunk(t, 0, True)
                    chunk(t, 1, True)
                if h == 0:
                    for b in range(2):
                        sp.wait_ge(s_kvl[h], (NCH - 1 + b) * (CI // SI[h]))
                        store_v(NCH - 2 + b, b, True)

            def load_v(n):
                k, r0 = n % 4, n * RI
                sp.dma_start(V0[k], v0_dram[:, r0:r0 + RI, :].rearrange("j r (s e) -> j r s e", s=2)
                             ).then_inc(s_vl[k], 16)
                sp.dma_start(V1[k], v1_dram[:, :, r0:r0 + RI, :].rearrange("s j r e -> (s j) r e")
                             ).then_inc(s_vl[k], 16)

            def load_x(n):
                k, rows = n % 3, slice(n * RI, (n + 1) * RI)
                sp.dma_start(XO[k][:, 0, :, :], xs[rows, 0:P, :].rearrange("r i e -> i r e")).then_inc(s_xl[k], 16)
                sp.dma_start(XO[k][0:E1, 1, :, :], xs[rows, P:C, :].rearrange("r i e -> i r e")
                             ).then_inc(s_xl[k], 16)

            for b in range(2):
                sp.wait_ge(s_vs[b], 32 * (NCH // 2))
            for k, then in enumerate(((), (load_v,), (load_x, load_v), (), (load_x, load_v), (load_v, load_x))):
                if then:
                    sp.wait_ge(s_qk[1], k + 1)
                for load in then:
                    load(placed[load.__name__])
                    placed[load.__name__] += 1
            for n in range(NRC):
                k, rows = n % 3, slice(n * RI, (n + 1) * RI)
                if n + 4 < NRC:
                    sp.wait_ge(s_av, BPC * (n + 1))
                    load_v(n + 4)
                sp.wait_ge(s_ad, BPC * (n + 1))
                sp.dma_start(outs[rows, 0:P, :].rearrange("r i e -> i r e"), XO[k][:, 0, :, :]
                             ).then_inc(s_out[k], 16)
                sp.wait_ge(s_lo, BPC // 2 * (n + 1))
                sp.dma_start(outs[rows, P:C, :].rearrange("r i e -> i r e"), XO[k][0:E1, 1, :, :]
                             ).then_inc(s_out[k], 16)
                if 0 < n < NRC - 2:
                    sp.wait_ge(s_out[(n - 1) % 3], 32 * ((n - 1) // 3 + 1))
                    load_x(n + 2)
            for k in range(3):
                sp.wait_ge(s_out[k], 32 * len(range(k, NRC, 3)))

        @block.gpsimd
        def _(pool):
            pool.memset(ident[:, :], 0.0).then_inc(s_zero, 1)
            pool.memset(ones[:, :], 1.0).then_inc(s_const, 1)
            pool.memset(UH1.bitcast(fp32), 0.0).then_inc(s_const, 1)
            pool.memset(UL1.bitcast(fp32), 0.0).then_inc(s_const, 1)
            pool.memset(res_i[:, :], 1).then_inc(s_zero, 1)
            pool.wait_ge(s_zero, 2)
            pool.affine_select(out=ident[:, :], in_=ident[:, :], compare_op=ALU.not_equal, fill=1.0,
                               base=0, pattern=[[-1, P]], channel_multiplier=1).then_inc(s_const, 1)
            pool.wait_ge(s_wh, 1)
            for col0, w, w0, n in W_PARTS:
                pool.tensor_tensor(WP[:, 1, :, col0:col0 + n], W[:, w, :, w0:w0 + n],
                                   WP[:, 0, :, col0:col0 + n], ALU.subtract).then_inc(s_wl, 1)
            for c in range(NCH):
                pool.wait_ge(s_h, c + 1)
                pool.tensor_tensor(TT[c][:, 1:3, 1, :], XN[c % 3][:, 1:3, :], TT[c][:, 1:3, 0, :],
                                   ALU.subtract).then_inc(s_l, 1)
            for h in range(2):
                for t0, t1, low in REGIONS:
                    with pool.Fori(t0, t1) as t:
                        for g in range(SPT[h]):
                            n = SPT[h] * t + g
                            pool.wait_ge(s_qh[h], n + 1)
                            pool.tensor_tensor(QA[:, :, bass.ds(SI[h] * n + low, SI[h])], TQ[h][g % 4],
                                               QA[:, :, bass.ds(SI[h] * n, SI[h])],
                                               ALU.subtract).then_inc(s_ql[h], 1)
            for n in range(NRC):
                for hp in range(HALF):
                    m = n * HALF + hp
                    pool.wait_ge(s_ol, m + 1)
                    pool.wait_ge(s_ad, 2 * m + 2)
                    o = XO[n % 3][0:E1, 1, :, hp * 2 * D:(hp + 1) * 2 * D]
                    pool.tensor_tensor(o, o, OLOW[m % 3][0:E1, :].rearrange("p (r e) -> p r e", r=RI),
                                       ALU.add).then_inc(s_lo, 1)

        @block.scalar
        def _(act):
            act.wait_ge(s_zero, 2)
            for k, w in enumerate((wq, wk, wv, wqs, wks)):
                act.dma_start(W[:, k, 0, :], w[0:P, :]).then_inc(s_params, 16)
                act.dma_start(W[0:E1, k, 1, :], w[P:E, :]).then_inc(s_params, 16)
                act.dma_start(W[E1:P, k, 1, :], w[P:E, :]).then_inc(s_params, 16)
            act.dma_start(X0[:, 0, :], xs[0, 0:P, :]).then_inc(s_params, 16)
            act.dma_start(X0[0:E1, 1, :], xs[0, P:C, :]).then_inc(s_params, 16)
            act.dma_start(seq_i[:, :], seq_mask.rearrange("a r -> r a")).then_inc(s_params, 16)
            act.dma_start(res_i[:, 0:1], res_mask[:, 0:P].rearrange("a r -> r a")).then_inc(s_params, 16)
            act.dma_start(res_i[0:E1, 1:2], res_mask[:, P:C].rearrange("a r -> r a")).then_inc(s_params, 16)
            act.dma_start(row_i, res_mask.partition_broadcast(P).rearrange("p a r -> p (a r)")
                          ).then_inc(s_params, 16)
            act.wait_ge(s_wsc, 1)
            for col0, w, w0, n in W_PARTS:
                ins = nc.scalar.copy(WP[:, 0, :, col0:col0 + n], W[:, w, :, w0:w0 + n])
            ins.then_inc(s_wh, 1)
            act.wait_ge(s_var, 1)
            nc.scalar.activation(t_n, var, ACT.Sqrt).then_inc(s_std, 1)
            act.wait_ge(s_const, 4)
            for k in range(3):
                act.wait_ge(s_u, k + 1)
                pu = PS[:, 4 * (k % 2):4 * (k % 2) + 4, :]
                u_out(nc.scalar, pu, k, True).then_inc(s_uh, 1)
            def xn_high(c):
                act.wait_ge(s_xn, c + 1)
                act.wait_ge(s_xc, c + 1)
                nc.scalar.copy(TT[c][:, :, 0, :], XN[c % 3]).then_inc(s_h, 1)

            act.wait_ge(s_ul, 3)
            act.wait_ge(s_wl, len(W_PARTS))
            for c in range(NCH):
                act.wait_ge(s_tr, c + 1)
                when(act, s_l, c - 2)
                when(act, s_ld, c - 2)
                nc.scalar.activation(XN[c % 3][:, 2, :], PS[:, 3 * (c % 2) + 2, :], ACT.Identity,
                                     bias=abc[:, 5:6], scale=abc[:, 2:3]).then_inc(s_xc, 1)
                if c:
                    xn_high(c - 1)
            xn_high(NCH - 1)
            act.wait_ge(s_ssh, 1)
            nc.scalar.activation(FLAT, FLAT, ACT.Exp).then_inc(s_sex, 1)
            act.wait_ge(s_swt, 1)
            nc.scalar.copy(SW[:, :], PS[:, 0:5, :].rearrange("p a b -> p (a b)")[:, 0:C * H]).then_inc(s_sw, 1)

            for h in range(2):
                def q_high(n, g):
                    act.wait_ge(s_tq[h], n + 1)
                    nc.scalar.copy(QA[:, :, bass.ds(SI[h] * n, SI[h])], TQ[h][g % 4]).then_inc(s_qh[h], 1)

                def body(t):
                    for g in range(SPT[h]):
                        n = SPT[h] * t + g
                        ps = projected(h, g)
                        b, at = divmod(g * SI[h], CI)
                        act.wait_ge(s_pj[h], n + 1)
                        if h == 0:
                            if at == 0:
                                when(act, s_vs[b], 32 * t)
                            nc.scalar.copy(VS[b][:, at:at + SI[h], 0:E],
                                           ps[:, :, 2 * EH:2 * EH + E]).then_inc(s_kvh[h], 1)
                        nc.scalar.copy(KA[:, :, bass.ds(SI[h] * n, SI[h])],
                                       ps[:, :, EH:2 * EH].rearrange("p i m -> p m i")).then_inc(s_kvh[h], 1)
                        if g or not isinstance(t, int):
                            q_high(n - 1, g - 1)

                body(0)
                with act.Fori(1, NCH // 2) as t:
                    body(t)
                q_high(NG[h] - 1, SPT[h] - 1)

                for b in range(2):
                    act.wait_ge(s_vs[b], 32 * (NCH // 2))

                def attention_high(k):
                    act.wait_ge(s_att[h], k + 1)
                    nc.scalar.copy(AT[h][:, k, :, 0:C],
                                   PS[:, 4 + k % 2, 0:2 * C].rearrange("p (t n) -> p t n", t=2)
                                   ).then_inc(s_ath[h], 1)

                for k in range(HALF):
                    act.wait_ge(s_qk[h], k + 1)
                    when(act, s_lr[h], k - 1)
                    nc.scalar.copy(LLOW[k % 2][0:E1, :], PS[E1:P, 2 * (k % 2) + 1, 0:C]).then_inc(s_ll[h], 1)
                    act.wait_ge(s_ls[h], k + 1)
                    nc.scalar.activation(LG[k % 2][:, :, 0:C], LG[k % 2][:, :, 0:C], ACT.Exp).then_inc(s_le[h], 1)
                    if k:
                        attention_high(k - 1)
                attention_high(HALF - 1)
            for m in range(NRC * HALF):
                act.wait_ge(s_av, 2 * m + 2)
                when(act, s_lo, m - 2)
                nc.scalar.activation(OLOW[m % 3][0:E1, :], PS[E1:P, (2 * m + 1) % 8, :], ACT.Copy,
                                     scale=mxb[0:E1, WV:WV + 1]).then_inc(s_ol, 1)

        @block.vector
        def _(dve):
            v = nc.vector
            count = [0]

            def step(ins):
                count[0] += 1
                ins.then_inc(s_dve, 1)
                dve.wait_ge(s_dve, count[0])

            dve.wait_ge(s_const, 4)
            dve.wait_ge(s_params, 16 * N_PARAMS)
            v.tensor_scalar(res01, res_i[:, :], 0, None, ALU.not_equal)
            v.tensor_scalar(seq01, seq_i[:, :], 0, None, ALU.not_equal)
            step(v.tensor_scalar(row01, row_i, 0, None, ALU.not_equal))
            v.tensor_scalar(M01[:, 0, :], row01, res01[:, 0:1], None, ALU.mult)
            step(v.tensor_scalar(seqneg, seq01, -1.0, FMAX, ALU.add, ALU.mult))
            step(v.tensor_scalar(M01[:, 1, :], row01, res01[:, 1:2], None, ALU.mult))
            v.tensor_scalar(NEG[:, :, :], M01[:, :, :], -1.0, FMAX, ALU.add, ALU.mult)
            v.tensor_reduce(parity, ident[:, :].rearrange("p (g a s) -> p a g s", a=2, s=D), AX.XY, ALU.add)
            v.tensor_reduce(mx5, W.rearrange("p w t n -> p w (t n)"), AX.X, ALU.max,
                            apply_absolute_value=True).then_inc(s_wmax, 1)
            dve.wait_ge(s_wmaxT, 1)
            step(v.tensor_reduce(m5t[0:5, :], PS[0:5, 0, 0:P], AX.X, ALU.max))
            v.tensor_scalar(d5[0:5, :], ident[0:5, 0:5], m5t[0:5, :], None, ALU.mult).then_inc(s_wd, 1)
            dve.wait_ge(s_wb, 1)
            step(v.tensor_scalar(mxb, PS[:, 1, 0:5], 1e-30, None, ALU.max))
            step(v.reciprocal(rv5, mxb))
            v.tensor_tensor(W.rearrange("p w t n -> p w (t n)"), W.rearrange("p w t n -> p w (t n)"),
                            rv5.unsqueeze(2).to_broadcast([P, 5, 2 * E]), ALU.mult).then_inc(s_wsc, 1)
            step(v.tensor_tensor(alpha, mxb[:, WQ:WQ + 1], mxb[:, WK:WK + 1], ALU.mult))
            step(v.tensor_scalar(alpha, alpha, 0.17677669529663687 / C ** 0.5 / SW_SCALE, None, ALU.mult))
            step(v.tensor_tensor(seqscale, mxb[:, WQS:WQS + 1], mxb[:, WKS:WKS + 1], ALU.mult))
            step(v.tensor_scalar(seqscale, seqscale, seq01, 1.0 / D ** 0.5 / U_SCALE, ALU.mult, ALU.mult))
            dve.wait_ge(s_wkt, 1)
            v.tensor_copy(WKT[:, 0, :], PS[:, 2, 0:256])
            step(v.tensor_copy(WKT[0:E1, 1, :], PS[0:E1, 2, 256:512]))
            for c in range(NXC):
                dve.wait_ge(s_x[c], 16)
                xv = X[:, c * XC * E:(c + 1) * XC * E].rearrange("p (i e) -> p i e", e=E)
                for g in range(G):
                    ins = v.bn_stats(ST[:, g, c, :], xv[:, :, g * GC:(g + 1) * GC])
            step(ins)
            sv = ST.rearrange("p g c (a s) -> p g (c a) s", s=3)
            K = 2 * NXC
            n_sub = XC * GC // 2
            v.tensor_reduce(s1, sv[:, :, :, 1], AX.X, ALU.add).then_inc(s_st1, 1)
            step(v.tensor_reduce(s3, sv[:, :, :, 2], AX.X, ALU.add))
            dve.wait_ge(s_mm1, 1)
            step(v.tensor_scalar(mean, PS[:, 1, 0:G], 1.0 / (K * R), None, ALU.mult))
            step(v.tensor_tensor(DM, sv[:, :, :, 1], mean.unsqueeze(2).to_broadcast([P, G, K]), ALU.subtract))
            step(v.tensor_tensor(DM, DM, DM, ALU.mult))
            step(v.tensor_reduce(s2, DM, AX.X, ALU.add))
            v.scalar_tensor_tensor(s2, s2, float(n_sub), s3, ALU.mult, ALU.add).then_inc(s_st2, 1)
            dve.wait_ge(s_mm2, 1)
            v.tensor_scalar(var, PS[:, 0, 0:G], 1.0 / (n_sub * K * R), EPS, ALU.mult,
                            ALU.add).then_inc(s_var, 1)
            dve.wait_ge(s_std, 1)
            step(v.reciprocal(y, t_n))
            step(v.tensor_tensor(t_n, y, y, ALU.mult))
            step(v.tensor_tensor(t_n, t_n, var, ALU.mult))
            step(v.tensor_scalar(t_n, t_n, -0.5, 1.5, ALU.mult, ALU.add))
            step(v.tensor_tensor(y, y, t_n, ALU.mult))
            step(v.scalar_tensor_tensor(y2, mean, -1.0, y, ALU.mult, ALU.mult))
            for k, q in enumerate((y, y2)):
                step(v.tensor_copy(AB[:, k, 0:E].rearrange("p (g s) -> p g s", s=GC),
                                   q.unsqueeze(2).to_broadcast([P, G, GC])))
            v.tensor_copy(AB[:, :, E:256], AB[:, :, 0:E1]).then_inc(s_ab, 1)
            dve.wait_ge(s_abT, 1)
            step(v.tensor_copy(abc, PS[:, 1, 0:6]))
            v.tensor_scalar(QX[:, 0, :], PS[:, 3, 0:C], abc[:, 0:1], abc[:, 3:4], ALU.mult, ALU.add)
            v.tensor_scalar(QX[0:E1, 1, :], PS[0:E1, 3, C:2 * C], abc[0:E1, 1:2], abc[0:E1, 4:5],
                            ALU.mult, ALU.add).then_inc(s_x0n, 1)
            dve.wait_ge(s_qs, 1)
            for a in range(2):
                v.tensor_scalar(QM[:, 0, a, :], PS[:, 0, 0:C], parity[:, a:a + 1], None, ALU.mult)
            for a in range(2):
                ins = v.tensor_scalar(QM[0:E1, 1, a, :], PS[0:E1, 0, C:2 * C], parity[0:E1, a:a + 1], None,
                                      ALU.mult)
            ins.then_inc(s_qm, 1)
            for k in range(3):
                dve.wait_ge(s_uh, k + 1)
                u_out(v, PS[:, 4 * (k % 2):4 * (k % 2) + 4, :], k, False).then_inc(s_ul, 1)

            def score(c):
                dve.wait_ge(s_sc, c + 1)
                v.tensor_scalar(SW[:, c * CI * H:(c + 1) * CI * H], PS[:, 6 + c % 2, 0:CI * H],
                                seqscale, seqneg, ALU.mult, ALU.add).then_inc(s_se, 1)

            def low(c):
                dve.wait_ge(s_h, c + 1)
                v.tensor_tensor(TT[c][:, 0, 1, :], XN[c % 3][:, 0, :], TT[c][:, 0, 0, :],
                                ALU.subtract).then_inc(s_ld, 1)

            dve.wait_ge(s_wl, len(W_PARTS))
            for c in range(NCH):
                dve.wait_ge(s_tr, c + 1)
                when(dve, s_l, c - 2)
                when(dve, s_ld, c - 2)
                for k in range(2):
                    ins = v.tensor_scalar(XN[c % 3][:, k, :], PS[:, 3 * (c % 2) + k, :], abc[:, k:k + 1],
                                          abc[:, 3 + k:4 + k], ALU.mult, ALU.add)
                ins.then_inc(s_xn, 1)
                if c >= 2:
                    low(c - 2)
                if c >= 4:
                    score(c - 4)
            low(NCH - 2)
            low(NCH - 1)
            for c in range(NCH - 4, NCH):
                score(c)
            flat = FLAT.rearrange("p (k r) -> p k r", r=R)
            st = PS[:, 0:5, :].rearrange("p a b -> p (a b)")[:, 0:C * H].rearrange("p (k r) -> p k r", r=R)
            dve.wait_ge(s_stt, 1)
            step(v.tensor_reduce(smx, st, AX.X, ALU.max))
            v.tensor_tensor(flat, st, smx.unsqueeze(2).to_broadcast([P, 18, R]), ALU.subtract).then_inc(s_ssh, 1)
            dve.wait_ge(s_sex, 1)
            step(v.tensor_reduce(ssum, flat, AX.X, ALU.add))
            step(v.reciprocal(sinv, ssum))
            step(v.tensor_scalar(sinv, sinv, SW_SCALE, None, ALU.mult))
            v.tensor_tensor(flat, flat, sinv.unsqueeze(2).to_broadcast([P, 18, R]), ALU.mult).then_inc(s_snm, 1)
            dve.wait_ge(s_sw, 1)

            for h in range(2):
                def body(t):
                    for g in range(SPT[h]):
                        n = SPT[h] * t + g
                        si = SI[h]
                        ps = projected(h, g)
                        b, at = divmod(g * si, CI)
                        dve.wait_ge(s_kvh[h], (2 - h) * (n + 1))
                        when(dve, s_ql[h], n - 3)
                        swv = SW[:, bass.ds(si * n * H, si * H)].rearrange("p (i m) -> p m i", m=H)
                        swv = swv[:, h * HALF:(h + 1) * HALF, :]
                        v.tensor_tensor(TQ[h][g % 4].rearrange("p (m d) i -> p m d i", d=D),
                                        ps[:, :, 0:EH].rearrange("p i (m d) -> p m d i", d=D),
                                        swv.unsqueeze(2).to_broadcast([P, HALF, D, si]),
                                        ALU.mult).then_inc(s_tq[h], 1)
                        if h == 0:
                            vs = VS[b][:, at:at + si, :]
                            v.tensor_tensor(vs[:, :, E:2 * E], ps[:, :, 2 * EH:2 * EH + E], vs[:, :, 0:E],
                                            ALU.subtract)
                        v.tensor_tensor(KA[:, :, bass.ds(si * n + C, si)],
                                        ps[:, :, EH:2 * EH].rearrange("p i m -> p m i"),
                                        KA[:, :, bass.ds(si * n, si)], ALU.subtract).then_inc(s_kvl[h], 1)

                body(0)
                with dve.Fori(1, NCH // 2) as t:
                    body(t)

                dve.wait_ge(s_ql[h], NG[h])
                for b in range(2):
                    v.memset(LG[b][E1:P, 1, :], 0.0)

                def attention_low(k):
                    dve.wait_ge(s_ath[h], k + 1)
                    pa = PS[:, 4 + k % 2, 0:2 * C].rearrange("p (t n) -> p t n", t=2)
                    for lo, hi, to in ((P, C, C), (0, P, C + E1)):
                        ins = v.tensor_tensor(AT[h][:, k, :, to:to + hi - lo], pa[:, :, lo:hi],
                                              AT[h][:, k, :, lo:hi], ALU.subtract)
                    ins.then_inc(s_atl[h], 1)

                for k in range(HALF):
                    lg = LG[k % 2]
                    lv = lg[:, :, 0:C]
                    dve.wait_ge(s_qk[h], k + 1)
                    when(dve, s_att[h], k - 1)
                    v.scalar_tensor_tensor(lg[:, 0, 0:C], PS[:, 2 * (k % 2), 0:C], alpha, M01[:, 0, :],
                                           ALU.mult, ALU.mult)
                    dve.wait_ge(s_ll[h], k + 1)
                    ins = v.tensor_tensor(lg[0:E1, 1, 0:C], PS[0:E1, 2 * (k % 2) + 1, 0:C],
                                          LLOW[k % 2][0:E1, :], ALU.add)
                    ins.then_inc(s_lr[h], 1)
                    dve.wait_ge(s_lr[h], k + 1)
                    step(v.scalar_tensor_tensor(lg[0:E1, 1, 0:C], lg[0:E1, 1, 0:C], alpha[0:E1, :],
                                                M01[0:E1, 1, :], ALU.mult, ALU.mult))
                    step(v.tensor_tensor(lv, lv, NEG[:, :, :], ALU.add))
                    step(v.tensor_reduce(lmx, lv, AX.X, ALU.max))
                    v.tensor_tensor(lv, lv, lmx.unsqueeze(2).to_broadcast([P, 2, C]),
                                    ALU.subtract).then_inc(s_ls[h], 1)
                    dve.wait_ge(s_le[h], k + 1)
                    step(v.tensor_reduce(lsum, lv, AX.X, ALU.add))
                    step(v.reciprocal(linv, lsum))
                    step(v.tensor_tensor(lg[:, :, C:256], lg[:, :, P:C],
                                         linv.unsqueeze(2).to_broadcast([P, 2, E1]), ALU.mult))
                    v.tensor_tensor(lv, lv, linv.unsqueeze(2).to_broadcast([P, 2, C]),
                                    ALU.mult).then_inc(s_at[h], 1)
                    if k:
                        attention_low(k - 1)
                attention_low(HALF - 1)

            for m in range(NRC * BPC):
                n, hp, t = m // BPC, m // 2 % HALF, m % 2
                if m % BPC == 0:
                    dve.wait_ge(s_xl[n % 3], 32 * (n // 3 + 1))
                rows = E1 if t else P
                dve.wait_ge(s_av, m + 1)
                o = XO[n % 3][0:rows, t, :, hp * 2 * D:(hp + 1) * 2 * D]
                v.scalar_tensor_tensor(o, PS[0:rows, m % 8, :].rearrange("p (r e) -> p r e", r=RI),
                                       mxb[0:rows, WV:WV + 1], o, ALU.mult, ALU.add).then_inc(s_ad, 1)

        @block.tensor
        def _(pe):
            mm = nc.tensor.matmul
            pe.wait_ge(s_const, 4)
            pe.wait_ge(s_wmax, 1)
            nc.tensor.transpose(PS[0:5, 0, 0:P], mx5, ident[:, :]).then_inc(s_wmaxT, 1)
            pe.wait_ge(s_wd, 1)
            mm(PS[:, 1, 0:5], ones[0:5, :], d5[0:5, :], start=True, stop=True).then_inc(s_wb, 1)
            pe.wait_ge(s_wsc, 1)
            nc.tensor.transpose(PS[:, 2, 0:P], W[:, WKS, 0, 0:P], ident[:, :])
            nc.tensor.transpose(PS[:, 2, P:E], W[0:E1, WKS, 1, 0:P], ident[0:E1, 0:E1])
            nc.tensor.transpose(PS[:, 2, E:256], W[0:E1, WKS, 0, 0:P], ident[0:E1, 0:E1])
            nc.tensor.transpose(PS[0:E1, 2, 256:384], W[:, WKS, 0, P:E], ident[:, :])
            nc.tensor.transpose(PS[0:E1, 2, 384:448], W[0:E1, WKS, 1, P:E], ident[0:E1, 0:E1])
            nc.tensor.transpose(PS[0:E1, 2, 448:512], W[0:E1, WKS, 0, P:E], ident[0:E1, 0:E1])
            nc.tensor.transpose(PS[:, 3, 0:P], X0[:, 0, 0:P], ident[:, :])
            nc.tensor.transpose(PS[:, 3, P:C], X0[0:E1, 1, 0:P], ident[0:E1, 0:E1])
            nc.tensor.transpose(PS[0:E1, 3, C:C + P], X0[:, 0, P:E], ident[:, :])
            nc.tensor.transpose(PS[0:E1, 3, C + P:2 * C], X0[0:E1, 1, P:E], ident[0:E1, 0:E1]).then_inc(s_wkt, 1)
            pe.wait_ge(s_st1, 1)
            mm(PS[:, 1, 0:G], ones[:, :], s1, start=True, stop=True).then_inc(s_mm1, 1)
            pe.wait_ge(s_st2, 1)
            mm(PS[:, 0, 0:G], ones[:, :], s2, start=True, stop=True).then_inc(s_mm2, 1)
            pe.wait_ge(s_ab, 1)
            for k in range(2):
                for t, e0 in enumerate((0, P, E1)):
                    ins = mm(PS[:, 1, 3 * k + t:3 * k + t + 1], AB[0:1, k, e0:e0 + P],
                             ones[0:1, 0:1], start=True, stop=True)
            ins.then_inc(s_abT, 1)
            pe.wait_ge(s_x0n, 1)
            for m, (lo, n) in enumerate(((0, P), (P, E1))):
                po = PS[0:n, 0, m * C:(m + 1) * C]
                mm(po, W[:, WQS, 0, lo:lo + n], QX[:, 0, :], start=True, stop=False)
                ins = mm(po, W[0:E1, WQS, 1, lo:lo + n], QX[0:E1, 1, :], start=False, stop=True)
            ins.then_inc(s_qs, 1)
            pe.wait_ge(s_qm, 1)
            for hd in range(H):
                t, row, par, k = hd // 8, 32 * ((hd % 8) // 2), hd % 2, hd // 4
                if hd % 4 == 0 and k >= 2:
                    pe.wait_ge(s_ul, k - 1)
                bank = 4 * (k % 2) + hd % 4
                for o, n, e0, cols in ((0, C // 2, 0, QM[row:row + 32, t, par, 0:C:2]),
                                       (C // 2, C // 2, E1, QM[row:row + 32, t, par, 1:C:2]),
                                       (C, C, P, QM[row:row + 32, t, par, :])):
                    ins = mm(PS[:, bank, o:o + n], WKT[row:row + 32, t, e0:e0 + P], cols, start=True, stop=True)
                if hd % 4 == 3:
                    ins.then_inc(s_u, 1)
            pe.wait_ge(s_ul, 3)

            def scores(c):
                b = c % 2
                pe.wait_ge(s_l, c + 1)
                pe.wait_ge(s_ld, c + 1)
                when(pe, s_se, c - 1)
                first = True
                for q in range(CI // 2):
                    j = c * CI // 2 + q
                    for a in range(2):
                        for s, u in ((0, UH0), (0, UL0), (1, UH0)):
                            mm(PS[:, 6 + b, (2 * q + a) * H:(2 * q + a + 1) * H],
                               TT[c][:, 2 * a, s, q * P:(q + 1) * P],
                               u[:, (a * C // 2 + j) * H:(a * C // 2 + j + 1) * H],
                               start=first, stop=False, skip_group_check=True)
                            first = False
                    for s, u in ((0, UH1), (0, UL1), (1, UH1)):
                        ins = mm(PS[:, 6 + b, 2 * q * H:(2 * q + 2) * H], TT[c][:, 1, s, q * P:(q + 1) * P],
                                 u[:, j * 2 * H:(j + 1) * 2 * H], start=False, stop=True,
                                 skip_group_check=True)
                ins.then_inc(s_sc, 1)

            for c in range(NCH):
                b = c % 2
                when(pe, s_xn, c - 1)
                when(pe, s_xc, c - 1)
                for q in range(CI // 2):
                    for k in range(3):
                        at = (c * CI + 2 * q) * E + k * P
                        ins = nc.tensor.transpose(PS[:, 3 * b + k, q * P:(q + 1) * P], X[:, at:at + P],
                                                  ident[:, :])
                ins.then_inc(s_tr, 1)
                if c >= 3:
                    scores(c - 3)
            for c in range(NCH - 3, NCH):
                scores(c)
            pe.wait_ge(s_se, NCH)
            for k in range(18):
                ins = nc.tensor.transpose(PS[:, k // 4, (k % 4) * P:(k % 4 + 1) * P],
                                          SW[:, k * P:(k + 1) * P], ident[:, :])
            ins.then_inc(s_stt, 1)
            pe.wait_ge(s_snm, 1)
            for k in range(18):
                ins = nc.tensor.transpose(PS[:, k // 4, (k % 4) * P:(k % 4 + 1) * P],
                                          FLAT[:, k * P:(k + 1) * P], ident[:, :])
            ins.then_inc(s_swt, 1)
            pe.wait_ge(s_sw, 1)

            pe.wait_ge(s_wl, len(W_PARTS))
            for h in range(2):
                wc = slice(h * CW[0], h * CW[0] + CW[h])

                def body(t):
                    for g in range(SPT[h]):
                        n = SPT[h] * t + g
                        b, at = divmod(g * SI[h], CI)
                        if at == 0:
                            pe.wait_ge(s_xt[h][b], 32 * (t + 1))
                        when(pe, s_kvl[h], n - 3)
                        ps = projected(h, g)
                        for i in range(SI[h]):
                            il = at + i
                            po = ps[:, i, 0:CW[h]]
                            slot = (il % 2) * (CI // 2) + il // 2
                            xh0 = XT[b][:, slot * R:(slot + 1) * R]
                            xl0 = XT[b][:, (CI + slot) * R:(CI + slot + 1) * R]
                            x1 = XT[b][:, (2 * CI + slot) * R:(2 * CI + slot + 1) * R]
                            mm(po, xh0, WP[:, 0, 0, wc], start=True, stop=False)
                            mm(po, xh0, WP[:, 1, 0, wc], start=False, stop=False)
                            mm(po, xl0, WP[:, 0, 0, wc], start=False, stop=False)
                            mm(po, x1, WP[:, 0, 1, wc], start=False, stop=False)
                            ins = mm(po, x1, WP[:, 1, 1, wc], start=False, stop=True)
                        ins.then_inc(s_pj[h], 1)

                body(0)
                with pe.Fori(1, NCH // 2) as t:
                    body(t)

                def transposes(k):
                    lg = LG[k % 2]
                    pe.wait_ge(s_at[h], k + 1)
                    when(pe, s_atl[h], k - 1)
                    pb = PS[:, 4 + k % 2, :]
                    nc.tensor.transpose(pb[:, 0:P], lg[:, 0, 0:P], ident[:, :])
                    nc.tensor.transpose(pb[:, P:C], lg[0:E1, 1, 0:P], ident[0:E1, 0:E1])
                    nc.tensor.transpose(pb[:, C:C + P], lg[:, 0, P:256], ident[:, :])
                    nc.tensor.transpose(pb[:, C + P:2 * C], lg[0:E1, 1, P:256],
                                        ident[0:E1, 0:E1]).then_inc(s_att[h], 1)

                pe.wait_ge(s_ql[h], NG[h])
                pe.wait_ge(s_kvl[h], NG[h])
                for k in range(HALF):
                    when(pe, s_lr[h], k - 1)
                    for d in range(D):
                        m = k * D + d
                        first, last = d == 0, d == D - 1
                        p0, p1 = PS[:, 2 * (k % 2), 0:C], PS[:, 2 * (k % 2) + 1, 0:C]
                        kh, kl = KA[:, m, 0:C], KA[:, m, C:2 * C]
                        mm(p0, QA[:, m, 0:P], kh, start=first, stop=False)
                        mm(p0, QA[:, m, 0:P], kl, start=False, stop=False)
                        mm(p0, QA[:, m, 2 * P:3 * P], kh, start=False, stop=last)
                        mm(p1, QA[:, m, P:2 * P], kh, start=first, stop=False)
                        ins = mm(p1, QA[:, m, P:2 * P], kl, start=False, stop=last)
                    ins.then_inc(s_qk[h], 1)
                    if k:
                        transposes(k - 1)
                transposes(HALF - 1)

                pe.wait_ge(s_atl[h], HALF)

            for m in range(NRC * BPC):
                n, hp, t = m // BPC, m // 2 % HALF, m % 2
                if m % BPC == 0:
                    pe.wait_ge(s_vl[n % 4], 32 * (n // 4 + 1))
                when(pe, s_ad, m - 7)
                if t:
                    when(pe, s_ol, (m - 7) // 2)
                po = PS[:, m % 8, :].rearrange("p (r a d) -> p r a d", a=2, d=D)
                for a in range(2):
                    k = 2 * hp + a
                    at = AT[k // HALF][:, k % HALF, :, :]
                    v0, v1 = V0[n % 4][:, :, :, k * D:(k + 1) * D], V1[n % 4][:, :, k * D:(k + 1) * D]
                    if t == 0:
                        high, low = slice(0, P), slice(C + E1, 2 * C)
                        terms = ((at[:, 0, high], v0[:, :, 0, :]), (at[:, 0, high], v0[:, :, 1, :]),
                                 (at[:, 0, low], v0[:, :, 0, :]), (at[:, 1, high], v1), (at[:, 1, low], v1))
                    else:
                        both = slice(P, 2 * P)
                        terms = ((at[:, 0, both], v0[:, :, 0, :]), (at[:, 0, both], v0[:, :, 1, :]),
                                 (at[:, 1, both], v1))
                    for j, (stationary, moving) in enumerate(terms):
                        ins = mm(po[:, :, a, :], stationary, moving, start=j == 0, stop=j == len(terms) - 1)
                ins.then_inc(s_av, 1)


_INS = ["x", "L0_conv_Wq", "L0_conv_Wk", "L0_conv_Wv", "L0_conv_Wq_s", "L0_conv_Wk_s",
        "L0_conv_res_mask", "L0_conv_seq_mask"]


def kernel(**inputs):
    import numpy as _np
    import concourse.bacc as _bacc
    from concourse import mybir as _mybir
    from concourse.bass_utils import run_bass_kernel_spmd as _run

    nc = _bacc.Bacc("TRN2", target_bir_lowering=False, num_devices=1)
    arrays, args = {}, []
    for name in _INS:
        a = _np.ascontiguousarray(inputs[name])
        arrays[f"in_{name}"] = a
        args.append(nc.dram_tensor(f"in_{name}", a.shape, _mybir.dt.from_np(a.dtype), kind="ExternalInput").ap())
    args.append(nc.dram_tensor("out_x", (1, R, C, E), _mybir.dt.float32, kind="ExternalOutput").ap())
    row_column_attention(nc, *args)
    r = _run(nc, [arrays], core_ids=[0])
    return r.results[0]["out_x"]
```

```python
import concourse.bass as bass
from concourse import mybir
from contextlib import ExitStack

fp32 = mybir.dt.float32
fp16 = mybir.dt.float16
int32 = mybir.dt.int32
ALU = mybir.AluOpType
ACT = mybir.ActivationFunctionType
AX = mybir.AxisListType

R, C, E, H = 128, 192, 192, 12
D = E // H
G, GC = 32, E // 32
P = 128
E1 = E - P
HALF = H // 2
EH = HALF * D
FMAX = 3.4028234663852886e38
EPS = 1e-5
U_SCALE = 0.125
SW_SCALE = 2.0
CI = 8
SI = (2, 4)
NXT = (2, 4)
CW = (2 * EH + E, 2 * EH)
RI = 16
NRC = R // RI
NV = 5
NCH = C // CI
XC = 32
NXC = C // XC
WQ, WK, WV, WQS, WKS = range(5)


def row_column_attention(nc, x, wq, wk, wv, wqs, wks, res_mask, seq_mask, out):
    xs = x.rearrange("b r c e -> (b r) c e")
    outs = out.rearrange("b r c e -> (b r) c e")

    xt_dram = nc.dram_tensor("xt_scratch", [NCH // 2, P, 6 * CI * R], fp16, kind="Internal").ap()
    v0_dram = nc.dram_tensor("v0_scratch", [P, R, 2 * E], fp16, kind="Internal").ap()
    v1_dram = nc.dram_tensor("v1_scratch", [2, E1, R, E], fp16, kind="Internal").ap()

    ctx = ExitStack()
    with ctx:
        def sb(name, shape, dt=fp32):
            return ctx.enter_context(nc.sbuf_tensor(name, shape, dt))

        def sem(name):
            return ctx.enter_context(nc.semaphore(name))

        BIG = sb("BIG", [P, C * E])
        X = BIG[:, :]
        AR = C * E // 2
        QA = BIG[:, 0:AR].bitcast(fp16).rearrange("p (m s) -> p m s", s=2 * C)
        KA = BIG[:, AR:2 * AR].bitcast(fp16).rearrange("p (m s) -> p m s", s=2 * C)
        TT = [BIG[:, c * CI * E:(c + 1) * CI * E].bitcast(fp16).rearrange("p (s t n) -> p t s n", t=3, s=2)
              for c in range(NCH)]
        VN = 3 * RI * E // 2
        V0 = [BIG[:, k * VN:k * VN + RI * E].bitcast(fp16).rearrange("p (r s e) -> p r s e", s=2, e=E)
              for k in range(4)]
        V1 = [BIG[:, k * VN + RI * E:(k + 1) * VN].bitcast(fp16).rearrange("p (r e) -> p r e", e=E)
              for k in range(4)]
        XO = [BIG[:, AR + 2 * k * RI * E:AR + 2 * (k + 1) * RI * E].rearrange("p (t r e) -> p t r e", t=2, e=E)
              for k in range(3)]

        EXTRA = sb("EXTRA", [P, 10496])
        place = [0]

        def part(n):
            place[0] += n
            return EXTRA[:, place[0] - n:place[0]]

        UH0, UL0, UH1, UL1 = (part(C * H // 2).bitcast(fp16) for _ in range(4))
        after_u = place[0]
        XN = [part(CI * E).rearrange("p (t n) -> p t n", t=3) for _ in range(3)]
        place[0] = after_u
        ST = part(G * NXC * 6).rearrange("p (g c s) -> p g c s", g=G, c=NXC)
        X0 = part(2 * E).rearrange("p (t n) -> p t n", t=2)
        AB = part(2 * 256).rearrange("p (t n) -> p t n", t=2)
        row_i = part(C).bitcast(int32)
        DM = part(G * 2 * NXC).rearrange("p (g k) -> p g k", g=G)
        place[0] = after_u + 3 * CI * E
        WKT = part(2 * 256).rearrange("p (t n) -> p t n", t=2)
        QM = part(4 * C).rearrange("p (t a n) -> p t a n", t=2, a=2)
        place[0] = 0
        XT = [part(3 * CI * R // 2).bitcast(fp16) for _ in range(4)]
        VS = [q.rearrange("p (i s) -> p i s", s=2 * E) for q in XT[2:4]]
        at_first = place[0]
        FLAT = part(C * H)
        at_tq = place[0]
        TQ = [part(4 * EH) for _ in range(4)]
        TQ = [[q[:, 0:SI[h] * EH].rearrange("p (m i) -> p m i", i=SI[h]) for q in TQ] for h in range(2)]
        AT = [EXTRA[:, o:o + HALF * 2 * C].bitcast(fp16).rearrange("p (h t n) -> p h t n", h=HALF, t=2)
              for o in (at_first, 0)]
        place[0] = at_tq
        LG = [part(2 * 256).rearrange("p (t n) -> p t n", t=2) for _ in range(2)]
        LLOW = [part(C) for _ in range(2)]
        V0 = V0 + [EXTRA[:, HALF * 2 * C:HALF * 2 * C + RI * E].bitcast(fp16)
                   .rearrange("p (r s e) -> p r s e", s=2, e=E)]
        OLOW = [EXTRA[:, at_tq + k * 512:at_tq + (k + 1) * 512] for k in range(3)]

        SW = sb("SW", [P, C * H])
        V1 = V1 + [SW[:, 0:RI * E // 2].bitcast(fp16).rearrange("p (r e) -> p r e", e=E)]
        W = SW[:, 0:5 * 2 * E].rearrange("p (w t n) -> p w t n", w=5, t=2)
        QX = SW[:, 5 * 2 * E:6 * 2 * E].rearrange("p (t n) -> p t n", t=2)
        WP = sb("WP", [P, 2, 2, sum(CW)], fp16)
        ident = sb("ident", [P, P])
        ones = sb("ones", [P, P])
        M01 = sb("M01", [P, 2, C])
        NEG = sb("NEG", [P, 2, C])
        small = sb("small", [P, 512])
        sp = [0]

        def col(n):
            sp[0] += n
            return small[:, sp[0] - n:sp[0]]

        seq_i = sb("seq_i", [P, 1], int32)
        res_i = sb("res_i", [P, 2], int32)
        seq01, seqneg, seqscale = col(1), col(1), col(1)
        res01 = col(2)
        parity = col(2)
        mx5, m5t, mxb, rv5, d5 = col(5), col(1), col(5), col(5), col(5)
        alpha = col(1)
        s1, mean, s2, s3, var, y, t_n, y2 = (col(G) for _ in range(8))
        abc = col(6)
        smx, ssum, sinv = col(18), col(18), col(18)
        lmx, lsum, linv = col(2), col(2), col(2)
        row01 = M01[:, 1, :]

        PS = ctx.enter_context(nc.psum_tensor("PS", [P, 8, 512], fp32))

        s_x = [sem(f"x_loaded{c}") for c in range(NXC)]
        s_params = sem("params_loaded")
        STORES = 16 * 7
        N_PARAMS = 5 * 3 + 2 + 4
        s_zero = sem("tiles_zeroed")
        s_const = sem("constants_ready")
        s_dve = sem("vector_step")
        s_wmax = sem("weight_max_ready")
        s_wmaxT = sem("weight_max_transposed")
        s_wd = sem("weight_max_diagonal")
        s_wb = sem("weight_max_everywhere")
        s_rv = sem("weight_scales_ready")
        s_wsc = sem("weights_scaled")
        s_wh = sem("weight_highs_ready")
        s_wl = sem("weight_lows_ready")
        s_wkt = sem("wks_and_x0_transposed")
        s_st1 = sem("row_means_summed")
        s_mm1 = sem("means_added")
        s_st2 = sem("squares_summed")
        s_mm2 = sem("squares_added")
        s_var = sem("variance_ready")
        s_std = sem("deviation_ready")
        s_ab = sem("scale_shift_rows")
        s_abT = sem("scale_shift_columns_psum")
        s_x0n = sem("x0_normalised")
        s_qs = sem("row_queries_psum")
        s_qm = sem("row_queries_masked")
        s_u = sem("score_vectors_psum")
        s_uh = sem("score_vector_highs")
        s_ul = sem("score_vectors_split")
        s_tr = sem("x_transposed")
        s_xn = sem("xnT_ready")
        s_h = sem("xnT_highs")
        s_l = sem("xnT_lows")
        s_sp = sem("xnT_stored")
        s_xc = sem("xnT_odd_tile_ready")
        s_ld = sem("xnT_even_tile_lows")
        s_sc = sem("scores_psum")
        s_se = sem("scores_ready")
        s_stt = sem("scores_transposed")
        s_ssh = sem("scores_shifted")
        s_sex = sem("scores_exponent")
        s_snm = sem("row_weights_normalised")
        s_swt = sem("row_weights_psum")
        s_sw = sem("row_weights_ready")
        s_xt = [[sem(f"xt{h}_loaded{b}") for b in range(NXT[h])] for h in range(2)]
        s_pj = [sem(f"projected{h}") for h in range(2)]
        s_kvh = [sem(f"kv_highs{h}") for h in range(2)]
        s_kvl = [sem(f"kv_lows{h}") for h in range(2)]
        s_tq = [sem(f"weighted_q{h}") for h in range(2)]
        s_qh = [sem(f"q_highs{h}") for h in range(2)]
        s_ql = [sem(f"q_lows{h}") for h in range(2)]
        s_vs = [sem(f"v_stored{b}") for b in range(2)]
        s_qk = [sem(f"logits_psum{h}") for h in range(2)]
        s_ll = [sem(f"logits_low_part{h}") for h in range(2)]
        s_lr = [sem(f"logits_read{h}") for h in range(2)]
        s_ls = [sem(f"logits_shifted{h}") for h in range(2)]
        s_le = [sem(f"logits_exponent{h}") for h in range(2)]
        s_at = [sem(f"attention_ready{h}") for h in range(2)]
        s_att = [sem(f"attention_transposed{h}") for h in range(2)]
        s_ath = [sem(f"attention_highs{h}") for h in range(2)]
        s_atl = [sem(f"attention_lows{h}") for h in range(2)]
        s_vl = [sem(f"v_loaded{k}") for k in range(NV)]
        s_xl = [sem(f"residual_loaded{k}") for k in range(3)]
        s_av = sem("attended_psum")
        s_ad = sem("residual_added")
        s_ol = sem("attended_low_part")
        s_lo = sem("low_part_added")
        s_out = [sem(f"out_stored{k}") for k in range(3)]

        def when(eng, s, value):
            if not isinstance(value, int) or value > 0:
                eng.wait_ge(s, value)

        NG = [C // n for n in SI]
        SPT = [NXT[h] * CI // SI[h] for h in range(2)]
        TURNS = [NCH // n for n in NXT]

        def projected(h, g):
            ps = PS[:, 2 * (g % 4):2 * (g % 4) + 2, :]
            return ps if h == 0 else ps.rearrange("p a (b n) -> p (a b) n", b=2)

        REGIONS = [[(0, P // (n * CI), C + E1), (P // (n * CI), TURNS[h], E1)] for h, n in enumerate(NXT)]

        def u_out(eng, pu, k, high):
            for rows, dst_h, dst_l, n, src in (
                    (slice(0, P), UH0, UL0, H, lambda q: q[:, :, 0:C]),
                    (slice(0, E1), UH1, UL1, 2 * H, lambda q: q[:, :, C:2 * C:2]),
                    (slice(E1, P), UH1, UL1, 2 * H, lambda q: q[:, :, C + 1:2 * C:2])):
                off = 2 * k + (H if rows.start else 0)
                s = src(pu[rows]).rearrange("p h i -> p i h")
                dh = dst_h[rows].rearrange("p (i s) -> p i s", s=n)[:, :, off:off + 2]
                dl = dst_l[rows].rearrange("p (i s) -> p i s", s=n)[:, :, off:off + 2]
                if high:
                    ins = eng.activation(dh, s, ACT.Copy, scale=U_SCALE)
                else:
                    ins = eng.scalar_tensor_tensor(dl, s, U_SCALE, dh, ALU.mult, ALU.subtract)
            return ins

        W_PARTS = ((0, WQ, 0, EH), (EH, WK, 0, EH), (2 * EH, WV, 0, E),
                   (CW[0], WQ, EH, EH), (CW[0] + EH, WK, EH, EH))
        U_AT = [1, 2, 3, 4, 5, 6]
        scored_at, scored = {c: [] for c in range(NCH)}, 0
        for c in range(U_AT[-1] + 1, NCH):
            if 2 * scored + 2 <= c - 3:
                scored_at[c].append(scored)
                scored += 1
        scored_at[NCH] = list(range(scored, NCH // 2))
        PARTS = 3
        BLOCKS = C * H // P // PARTS
        PAIRS = NCH // 2 // PARTS

        def part_psum(p):
            return PS[:, 2 * p:2 * p + 2, :].rearrange("p a b -> p (a b)")[:, 0:BLOCKS * P]

        BUF = [4, 0, 1, 2, 3]
        BPC = H

        block = ctx.enter_context(nc.Block())

        @block.sync
        def _(sp):
            for c in range(NXC):
                if c == 1:
                    sp.wait_ge(s_params, 16 * N_PARAMS)
                sp.dma_start(X[:, c * XC * E:(c + 1) * XC * E],
                             xs[:, c * XC:(c + 1) * XC, :].rearrange("r c e -> r (c e)")).then_inc(s_x[c], 16)
            for c in range(0, NCH, 2):
                sp.wait_ge(s_l, c + 2)
                sp.wait_ge(s_ld, c + 2)
                full = xt_dram[c // 2, :, 0:4 * CI * R].rearrange("p (c a n) -> p c a n", a=2, n=512)
                rest = xt_dram[c // 2, :, 4 * CI * R:6 * CI * R].rearrange("p (c a n) -> p c a n", a=2, n=512)
                src = BIG[:, c * CI * E:(c + 2) * CI * E].bitcast(fp16)
                src = src.rearrange("p (c t n) -> p c t n", t=3, n=512)
                even, mixed, odd = (src[:, :, t, :] for t in range(3))
                sp.dma_start(full[:, :, 0, :], even).then_inc(s_sp, 16)
                sp.dma_start(full[0:E1, :, 1, :], mixed[E1:P]).then_inc(s_sp, 16)
                sp.dma_start(full[E1:P, :, 1, :], odd[0:E1]).then_inc(s_sp, 16)
                for s in range(2):
                    to = rest[s * E1:(s + 1) * E1]
                    sp.dma_start(to[:, :, 0, :], mixed[0:E1, s::2, :]).then_inc(s_sp, 16)
                    sp.dma_start(to[:, :, 1, :], odd[E1:P, s::2, :]).then_inc(s_sp, 16)
            sp.wait_ge(s_sc, NCH // 2)
            sp.wait_ge(s_sp, STORES * NCH // 2)
            def load_xt(h, pair, odd, b):
                src = xt_dram[bass.ds(pair, 1), :, :].rearrange("a p n -> p (a n)")
                n0, n1 = 2 * CI * R, 4 * CI * R
                sp.dma_start(XT[b][:, 0:n0], src[:, odd * n0:(odd + 1) * n0]).then_inc(s_xt[h][b], 16)
                sp.dma_start(XT[b][:, n0:], src[:, n1 + odd * CI * R:n1 + (odd + 1) * CI * R]
                             ).then_inc(s_xt[h][b], 16)

            def store_v(c, b, second):
                for k in range(2):
                    if not second:
                        cols = slice(k * CI // 2, (k + 1) * CI // 2)
                        sp.dma_start(v0_dram[bass.ds(c * CI + k * CI // 2, CI // 2), :, :]
                                     .rearrange("i r s -> r i s"), VS[b][:, cols, :]).then_inc(s_vs[b], 16)
                    else:
                        sp.dma_start(v1_dram[k, bass.ds(c * CI - P, CI), :, :].rearrange("i r s -> r i s"),
                                     VS[b][:, :, k * E:(k + 1) * E]).then_inc(s_vs[b], 16)

            def first(t, b, second):
                c = 2 * t + b
                sp.wait_ge(s_pj[0], (c - 1) * (CI // SI[0]))
                load_xt(0, t, b, b)
                sp.wait_ge(s_kvl[0], (c - 1) * (CI // SI[0]))
                store_v(c - 2, b, second)

            for b in range(2):
                load_xt(0, 0, b, b)
            for t0, t1, second in ((1, 9, False), (9, TURNS[0], True)):
                with sp.Fori(t0, t1) as t:
                    for b in range(2):
                        first(t, b, second)
            for b in range(2):
                sp.wait_ge(s_kvl[0], (NCH - 1 + b) * (CI // SI[0]))
                store_v(NCH - 2 + b, b, True)
            for b in range(4):
                if b == 2:
                    for k in range(2):
                        sp.wait_ge(s_vs[k], 32 * (NCH // 2))
                load_xt(1, b // 2, b % 2, b)
            with sp.Fori(1, TURNS[1]) as t:
                for b in range(4):
                    sp.wait_ge(s_pj[1], (4 * t + b - 3) * (CI // SI[1]))
                    load_xt(1, 2 * t + b // 2, b % 2, b)

            def load_v(n, parts=(0, 1)):
                k, r0 = BUF[n % NV], n * RI
                to = (V0[k], V1[k])
                of = (v0_dram[:, r0:r0 + RI, :].rearrange("j r (s e) -> j r s e", s=2),
                      v1_dram[:, :, r0:r0 + RI, :].rearrange("s j r e -> (s j) r e"))
                for t in parts:
                    sp.dma_start(to[t], of[t]).then_inc(s_vl[n % NV], 16)

            def load_x(n, parts=(0, 1)):
                k, rows = n % 3, slice(n * RI, (n + 1) * RI)
                to = (XO[k][:, 0, :, :], XO[k][0:E1, 1, :, :])
                of = (xs[rows, 0:P, :].rearrange("r i e -> i r e"), xs[rows, P:C, :].rearrange("r i e -> i r e"))
                for t in parts:
                    sp.dma_start(to[t], of[t]).then_inc(s_xl[k], 16)

            sp.wait_ge(s_pj[1], NG[1])
            sp.wait_ge(s_tq[1], NG[1])
            load_v(0)
            for k, loads in enumerate((((load_v, 1, 0), (load_x, 0, 0)),
                                       ((load_v, 1, 1), (load_x, 0, 1)),
                                       ((load_v, 2, 0), (load_v, 2, 1), (load_x, 1, 0)),
                                       ((load_v, 3, 0), (load_x, 1, 1)),
                                       ((load_v, 3, 1), (load_x, 2, 0)),
                                       ((load_v, 4, 0), (load_v, 4, 1), (load_x, 2, 1)))):
                sp.wait_ge(s_qk[1], k + 1)
                for load, n, t in loads:
                    load(n, (t,))
            for n in range(NRC):
                k, rows = n % 3, slice(n * RI, (n + 1) * RI)
                if n + NV < NRC:
                    sp.wait_ge(s_av, BPC * (n + 1))
                    load_v(n + NV)
                sp.wait_ge(s_ad, BPC * (n + 1))
                sp.dma_start(outs[rows, 0:P, :].rearrange("r i e -> i r e"), XO[k][:, 0, :, :]
                             ).then_inc(s_out[k], 16)
                sp.wait_ge(s_lo, BPC // 2 * (n + 1))
                sp.dma_start(outs[rows, P:C, :].rearrange("r i e -> i r e"), XO[k][0:E1, 1, :, :]
                             ).then_inc(s_out[k], 16)
                if 0 < n < NRC - 2:
                    sp.wait_ge(s_out[(n - 1) % 3], 32 * ((n - 1) // 3 + 1))
                    load_x(n + 2)
            for k in range(3):
                sp.wait_ge(s_out[k], 32 * len(range(k, NRC, 3)))

        @block.gpsimd
        def _(pool):
            pool.memset(ident[:, :], 0.0).then_inc(s_zero, 1)
            pool.memset(ones[:, :], 1.0).then_inc(s_const, 1)
            pool.memset(UH1.bitcast(fp32), 0.0).then_inc(s_const, 1)
            pool.memset(UL1.bitcast(fp32), 0.0).then_inc(s_const, 1)
            pool.memset(res_i[:, :], 1).then_inc(s_zero, 1)
            pool.wait_ge(s_zero, 2)
            pool.affine_select(out=ident[:, :], in_=ident[:, :], compare_op=ALU.not_equal, fill=1.0,
                               base=0, pattern=[[-1, P]], channel_multiplier=1).then_inc(s_const, 1)
            pool.wait_ge(s_wh, 1)
            for col0, w, w0, n in W_PARTS:
                pool.tensor_tensor(WP[:, 1, :, col0:col0 + n], W[:, w, :, w0:w0 + n],
                                   WP[:, 0, :, col0:col0 + n], ALU.subtract).then_inc(s_wl, 1)
            for c in range(NCH):
                pool.wait_ge(s_h, c + 1)
                pool.tensor_tensor(TT[c][:, 1:3, 1, :], XN[c % 3][:, 1:3, :], TT[c][:, 1:3, 0, :],
                                   ALU.subtract).then_inc(s_l, 1)
            for h in range(2):
                for t0, t1, low in REGIONS[h]:
                    with pool.Fori(t0, t1) as t:
                        for g in range(SPT[h]):
                            n = SPT[h] * t + g
                            pool.wait_ge(s_qh[h], n + 1)
                            pool.tensor_tensor(QA[:, :, bass.ds(SI[h] * n + low, SI[h])], TQ[h][g % 4],
                                               QA[:, :, bass.ds(SI[h] * n, SI[h])],
                                               ALU.subtract).then_inc(s_ql[h], 1)
            for n in range(NRC):
                for hp in range(HALF):
                    m = n * HALF + hp
                    pool.wait_ge(s_ol, m + 1)
                    pool.wait_ge(s_ad, 2 * m + 2)
                    o = XO[n % 3][0:E1, 1, :, hp * 2 * D:(hp + 1) * 2 * D]
                    pool.tensor_tensor(o, o, OLOW[m % 3][0:E1, :].rearrange("p (r e) -> p r e", r=RI),
                                       ALU.add).then_inc(s_lo, 1)

        @block.scalar
        def _(act):
            act.wait_ge(s_zero, 2)
            for k, w in enumerate((wq, wk, wv, wqs, wks)):
                act.dma_start(W[:, k, 0, :], w[0:P, :]).then_inc(s_params, 16)
                act.dma_start(W[0:E1, k, 1, :], w[P:E, :]).then_inc(s_params, 16)
                act.dma_start(W[E1:P, k, 1, :], w[P:E, :]).then_inc(s_params, 16)
            act.dma_start(X0[:, 0, :], xs[0, 0:P, :]).then_inc(s_params, 16)
            act.dma_start(X0[0:E1, 1, :], xs[0, P:C, :]).then_inc(s_params, 16)
            act.dma_start(seq_i[:, :], seq_mask.rearrange("a r -> r a")).then_inc(s_params, 16)
            act.dma_start(res_i[:, 0:1], res_mask[:, 0:P].rearrange("a r -> r a")).then_inc(s_params, 16)
            act.dma_start(res_i[0:E1, 1:2], res_mask[:, P:C].rearrange("a r -> r a")).then_inc(s_params, 16)
            act.dma_start(row_i, res_mask.partition_broadcast(P).rearrange("p a r -> p (a r)")
                          ).then_inc(s_params, 16)
            act.wait_ge(s_rv, 1)
            for k in range(5):
                ins = nc.scalar.mul(W[:, k, :, :], W[:, k, :, :], rv5[:, k:k + 1])
            ins.then_inc(s_wsc, 1)
            act.wait_ge(s_wsc, 1)
            for col0, w, w0, n in W_PARTS:
                ins = nc.scalar.copy(WP[:, 0, :, col0:col0 + n], W[:, w, :, w0:w0 + n])
            ins.then_inc(s_wh, 1)
            act.wait_ge(s_var, 1)
            nc.scalar.activation(t_n, var, ACT.Sqrt).then_inc(s_std, 1)
            def xn_high(c):
                act.wait_ge(s_xn, c + 1)
                act.wait_ge(s_xc, c + 1)
                nc.scalar.copy(TT[c][:, :, 0, :], XN[c % 3]).then_inc(s_h, 1)

            act.wait_ge(s_const, 4)
            act.wait_ge(s_x0n, 1)
            for c in range(NCH):
                act.wait_ge(s_tr, c + 1)
                when(act, s_l, c - 2)
                when(act, s_ld, c - 2)
                nc.scalar.activation(XN[c % 3][:, 2, :], PS[:, 3 * (c % 2) + 2, :], ACT.Identity,
                                     bias=abc[:, 5:6], scale=abc[:, 2:3]).then_inc(s_xc, 1)
                if c:
                    xn_high(c - 1)
                if c in U_AT:
                    k = U_AT.index(c)
                    act.wait_ge(s_u, k + 1)
                    u_out(nc.scalar, PS[:, 6:8, :], k, True).then_inc(s_uh, 1)
            xn_high(NCH - 1)
            for p in range(PARTS):
                act.wait_ge(s_ssh, p + 1)
                fp = FLAT[:, p * BLOCKS * R:(p + 1) * BLOCKS * R]
                nc.scalar.activation(fp, fp, ACT.Exp).then_inc(s_sex, 1)
            for p in range(PARTS):
                act.wait_ge(s_swt, p + 1)
                nc.scalar.copy(SW[:, p * BLOCKS * P:(p + 1) * BLOCKS * P], part_psum(p)).then_inc(s_sw, 1)

            for h in range(2):
                def q_high(n, g):
                    act.wait_ge(s_tq[h], n + 1)
                    nc.scalar.copy(QA[:, :, bass.ds(SI[h] * n, SI[h])], TQ[h][g % 4]).then_inc(s_qh[h], 1)

                def body(t):
                    for g in range(SPT[h]):
                        n = SPT[h] * t + g
                        ps = projected(h, g)
                        b, at = divmod(g * SI[h], CI)
                        act.wait_ge(s_pj[h], n + 1)
                        if h == 0:
                            if at == 0:
                                when(act, s_vs[b], 32 * t)
                            nc.scalar.copy(VS[b][:, at:at + SI[h], 0:E],
                                           ps[:, :, 2 * EH:2 * EH + E]).then_inc(s_kvh[h], 1)
                        nc.scalar.copy(KA[:, :, bass.ds(SI[h] * n, SI[h])],
                                       ps[:, :, EH:2 * EH].rearrange("p i m -> p m i")).then_inc(s_kvh[h], 1)
                        if g or not isinstance(t, int):
                            q_high(n - 1, g - 1)

                body(0)
                with act.Fori(1, TURNS[h]) as t:
                    body(t)
                q_high(NG[h] - 1, SPT[h] - 1)

                def attention_high(k):
                    act.wait_ge(s_att[h], k + 1)
                    nc.scalar.copy(AT[h][:, k, :, 0:C],
                                   PS[:, 4 + k % 2, 0:2 * C].rearrange("p (t n) -> p t n", t=2)
                                   ).then_inc(s_ath[h], 1)

                for k in range(HALF):
                    act.wait_ge(s_qk[h], k + 1)
                    when(act, s_lr[h], k - 1)
                    nc.scalar.copy(LLOW[k % 2][0:E1, :], PS[E1:P, 2 * (k % 2) + 1, 0:C]).then_inc(s_ll[h], 1)
                    act.wait_ge(s_ls[h], k + 1)
                    nc.scalar.activation(LG[k % 2][:, :, 0:C], LG[k % 2][:, :, 0:C], ACT.Exp).then_inc(s_le[h], 1)
                    if k:
                        attention_high(k - 1)
                attention_high(HALF - 1)
            for m in range(NRC * HALF):
                act.wait_ge(s_av, 2 * m + 2)
                when(act, s_lo, m - 2)
                nc.scalar.activation(OLOW[m % 3][0:E1, :], PS[E1:P, (2 * m + 1) % 8, :], ACT.Copy,
                                     scale=mxb[0:E1, WV:WV + 1]).then_inc(s_ol, 1)

        @block.vector
        def _(dve):
            v = nc.vector
            count = [0]

            def step(ins):
                count[0] += 1
                ins.then_inc(s_dve, 1)
                dve.wait_ge(s_dve, count[0])

            def statistics(c):
                dve.wait_ge(s_x[c], 16)
                xv = X[:, c * XC * E:(c + 1) * XC * E].rearrange("p (i e) -> p i e", e=E)
                for g in range(G):
                    ins = v.bn_stats(ST[:, g, c, :], xv[:, :, g * GC:(g + 1) * GC])
                return ins

            statistics(0)
            dve.wait_ge(s_const, 4)
            dve.wait_ge(s_params, 16 * N_PARAMS)
            v.tensor_scalar(res01, res_i[:, :], 0, None, ALU.not_equal)
            v.tensor_scalar(seq01, seq_i[:, :], 0, None, ALU.not_equal)
            step(v.tensor_scalar(row01, row_i, 0, None, ALU.not_equal))
            v.tensor_scalar(M01[:, 0, :], row01, res01[:, 0:1], None, ALU.mult)
            step(v.tensor_scalar(seqneg, seq01, -1.0, FMAX, ALU.add, ALU.mult))
            step(v.tensor_scalar(M01[:, 1, :], row01, res01[:, 1:2], None, ALU.mult))
            v.tensor_scalar(NEG[:, :, :], M01[:, :, :], -1.0, FMAX, ALU.add, ALU.mult)
            v.tensor_reduce(parity, ident[:, :].rearrange("p (g a s) -> p a g s", a=2, s=D), AX.XY, ALU.add)
            v.tensor_reduce(mx5, W.rearrange("p w t n -> p w (t n)"), AX.X, ALU.max,
                            apply_absolute_value=True).then_inc(s_wmax, 1)
            dve.wait_ge(s_wmaxT, 1)
            step(v.tensor_reduce(m5t[0:5, :], PS[0:5, 0, 0:P], AX.X, ALU.max))
            v.tensor_scalar(d5[0:5, :], ident[0:5, 0:5], m5t[0:5, :], None, ALU.mult).then_inc(s_wd, 1)
            dve.wait_ge(s_wb, 1)
            step(v.tensor_scalar(mxb, PS[:, 1, 0:5], 1e-30, None, ALU.max))
            v.reciprocal(rv5, mxb).then_inc(s_rv, 1)
            step(v.tensor_tensor(alpha, mxb[:, WQ:WQ + 1], mxb[:, WK:WK + 1], ALU.mult))
            step(v.tensor_scalar(alpha, alpha, 0.17677669529663687 / C ** 0.5 / SW_SCALE, None, ALU.mult))
            step(v.tensor_tensor(seqscale, mxb[:, WQS:WQS + 1], mxb[:, WKS:WKS + 1], ALU.mult))
            step(v.tensor_scalar(seqscale, seqscale, seq01, 1.0 / D ** 0.5 / U_SCALE, ALU.mult, ALU.mult))
            dve.wait_ge(s_wkt, 1)
            v.tensor_copy(WKT[:, 0, :], PS[:, 2, 0:256])
            step(v.tensor_copy(WKT[0:E1, 1, :], PS[0:E1, 2, 256:512]))
            for c in range(1, NXC):
                ins = statistics(c)
            step(ins)
            sv = ST.rearrange("p g c (a s) -> p g (c a) s", s=3)
            K = 2 * NXC
            n_sub = XC * GC // 2
            v.tensor_reduce(s1, sv[:, :, :, 1], AX.X, ALU.add).then_inc(s_st1, 1)
            step(v.tensor_reduce(s3, sv[:, :, :, 2], AX.X, ALU.add))
            dve.wait_ge(s_mm1, 1)
            step(v.tensor_scalar(mean, PS[:, 1, 0:G], 1.0 / (K * R), None, ALU.mult))
            step(v.tensor_tensor(DM, sv[:, :, :, 1], mean.unsqueeze(2).to_broadcast([P, G, K]), ALU.subtract))
            step(v.tensor_tensor(DM, DM, DM, ALU.mult))
            step(v.tensor_reduce(s2, DM, AX.X, ALU.add))
            v.scalar_tensor_tensor(s2, s2, float(n_sub), s3, ALU.mult, ALU.add).then_inc(s_st2, 1)
            dve.wait_ge(s_mm2, 1)
            v.tensor_scalar(var, PS[:, 0, 0:G], 1.0 / (n_sub * K * R), EPS, ALU.mult,
                            ALU.add).then_inc(s_var, 1)
            dve.wait_ge(s_std, 1)
            step(v.reciprocal(y, t_n))
            step(v.tensor_tensor(t_n, y, y, ALU.mult))
            step(v.tensor_tensor(t_n, t_n, var, ALU.mult))
            step(v.tensor_scalar(t_n, t_n, -0.5, 1.5, ALU.mult, ALU.add))
            step(v.tensor_tensor(y, y, t_n, ALU.mult))
            step(v.scalar_tensor_tensor(y2, mean, -1.0, y, ALU.mult, ALU.mult))
            for k, q in enumerate((y, y2)):
                step(v.tensor_copy(AB[:, k, 0:E].rearrange("p (g s) -> p g s", s=GC),
                                   q.unsqueeze(2).to_broadcast([P, G, GC])))
            v.tensor_copy(AB[:, :, E:256], AB[:, :, 0:E1]).then_inc(s_ab, 1)
            dve.wait_ge(s_abT, 1)
            step(v.tensor_copy(abc, PS[:, 7, 0:6]))
            v.tensor_scalar(QX[:, 0, :], PS[:, 6, 0:C], abc[:, 0:1], abc[:, 3:4], ALU.mult, ALU.add)
            v.tensor_scalar(QX[0:E1, 1, :], PS[0:E1, 6, C:2 * C], abc[0:E1, 1:2], abc[0:E1, 4:5],
                            ALU.mult, ALU.add).then_inc(s_x0n, 1)
            dve.wait_ge(s_qs, 1)
            for a in range(2):
                v.tensor_scalar(QM[:, 0, a, :], PS[:, 7, 0:C], parity[:, a:a + 1], None, ALU.mult)
            for a in range(2):
                ins = v.tensor_scalar(QM[0:E1, 1, a, :], PS[0:E1, 7, C:2 * C], parity[0:E1, a:a + 1], None,
                                      ALU.mult)
            ins.then_inc(s_qm, 1)

            def score(m):
                if m == 0:
                    dve.wait_ge(s_wl, len(W_PARTS))
                dve.wait_ge(s_sc, m + 1)
                v.tensor_scalar(SW[:, 2 * m * CI * H:2 * (m + 1) * CI * H], PS[:, 6 + m % 2, 0:2 * CI * H],
                                seqscale, seqneg, ALU.mult, ALU.add).then_inc(s_se, 1)

            def low(c):
                dve.wait_ge(s_h, c + 1)
                v.tensor_tensor(TT[c][:, 0, 1, :], XN[c % 3][:, 0, :], TT[c][:, 0, 0, :],
                                ALU.subtract).then_inc(s_ld, 1)

            for c in range(NCH):
                dve.wait_ge(s_tr, c + 1)
                when(dve, s_l, c - 2)
                when(dve, s_ld, c - 2)
                for k in range(2):
                    ins = v.tensor_scalar(XN[c % 3][:, k, :], PS[:, 3 * (c % 2) + k, :], abc[:, k:k + 1],
                                          abc[:, 3 + k:4 + k], ALU.mult, ALU.add)
                ins.then_inc(s_xn, 1)
                if c >= 2:
                    low(c - 2)
                if c in U_AT:
                    k = U_AT.index(c)
                    dve.wait_ge(s_uh, k + 1)
                    u_out(v, PS[:, 6:8, :], k, False).then_inc(s_ul, 1)
                for k in scored_at.get(c - 1, []):
                    score(k)
            low(NCH - 2)
            for m in scored_at[NCH - 1]:
                score(m)
            low(NCH - 1)

            def part(p):
                cols = slice(p * BLOCKS, (p + 1) * BLOCKS)
                return (FLAT.rearrange("p (k r) -> p k r", r=R)[:, cols, :], smx[:, cols], ssum[:, cols],
                        sinv[:, cols])

            for p in range(PARTS):
                flat, top, _, _ = part(p)
                st = part_psum(p).rearrange("p (k r) -> p k r", r=R)
                dve.wait_ge(s_stt, p + 1)
                step(v.tensor_reduce(top, st, AX.X, ALU.max))
                dve.wait_ge(s_l, NCH if p == PARTS - 1 else NCH - 1)
                v.tensor_tensor(flat, st, top.unsqueeze(2).to_broadcast([P, BLOCKS, R]),
                                ALU.subtract).then_inc(s_ssh, 1)
                if p < len(scored_at[NCH]):
                    score(scored_at[NCH][p])
            for p in range(PARTS):
                flat, _, total, inv = part(p)
                dve.wait_ge(s_sex, p + 1)
                step(v.tensor_reduce(total, flat, AX.X, ALU.add))
                step(v.reciprocal(inv, total))
                step(v.tensor_scalar(inv, inv, SW_SCALE, None, ALU.mult))
                v.tensor_tensor(flat, flat, inv.unsqueeze(2).to_broadcast([P, BLOCKS, R]),
                                ALU.mult).then_inc(s_snm, 1)
            dve.wait_ge(s_sw, 1)

            for h in range(2):
                def body(t):
                    for g in range(SPT[h]):
                        n = SPT[h] * t + g
                        si = SI[h]
                        ps = projected(h, g)
                        b, at = divmod(g * si, CI)
                        dve.wait_ge(s_kvh[h], (2 - h) * (n + 1))
                        when(dve, s_ql[h], n - 3)
                        swv = SW[:, bass.ds(si * n * H, si * H)].rearrange("p (i m) -> p m i", m=H)
                        swv = swv[:, h * HALF:(h + 1) * HALF, :]
                        v.tensor_tensor(TQ[h][g % 4].rearrange("p (m d) i -> p m d i", d=D),
                                        ps[:, :, 0:EH].rearrange("p i (m d) -> p m d i", d=D),
                                        swv.unsqueeze(2).to_broadcast([P, HALF, D, si]),
                                        ALU.mult).then_inc(s_tq[h], 1)
                        if h == 0:
                            vs = VS[b][:, at:at + si, :]
                            v.tensor_tensor(vs[:, :, E:2 * E], ps[:, :, 2 * EH:2 * EH + E], vs[:, :, 0:E],
                                            ALU.subtract)
                        v.tensor_tensor(KA[:, :, bass.ds(si * n + C, si)],
                                        ps[:, :, EH:2 * EH].rearrange("p i m -> p m i"),
                                        KA[:, :, bass.ds(si * n, si)], ALU.subtract).then_inc(s_kvl[h], 1)

                body(0)
                if h == 0:
                    dve.wait_ge(s_sw, PARTS)
                with dve.Fori(1, TURNS[h]) as t:
                    body(t)

                dve.wait_ge(s_ql[h], NG[h])
                for b in range(2):
                    v.memset(LG[b][E1:P, 1, :], 0.0)

                def attention_low(k):
                    dve.wait_ge(s_ath[h], k + 1)
                    pa = PS[:, 4 + k % 2, 0:2 * C].rearrange("p (t n) -> p t n", t=2)
                    for lo, hi, to in ((P, C, C), (0, P, C + E1)):
                        ins = v.tensor_tensor(AT[h][:, k, :, to:to + hi - lo], pa[:, :, lo:hi],
                                              AT[h][:, k, :, lo:hi], ALU.subtract)
                    ins.then_inc(s_atl[h], 1)

                for k in range(HALF):
                    lg = LG[k % 2]
                    lv = lg[:, :, 0:C]
                    dve.wait_ge(s_qk[h], k + 1)
                    when(dve, s_att[h], k - 1)
                    v.scalar_tensor_tensor(lg[:, 0, 0:C], PS[:, 2 * (k % 2), 0:C], alpha, M01[:, 0, :],
                                           ALU.mult, ALU.mult)
                    dve.wait_ge(s_ll[h], k + 1)
                    ins = v.tensor_tensor(lg[0:E1, 1, 0:C], PS[0:E1, 2 * (k % 2) + 1, 0:C],
                                          LLOW[k % 2][0:E1, :], ALU.add)
                    ins.then_inc(s_lr[h], 1)
                    dve.wait_ge(s_lr[h], k + 1)
                    step(v.scalar_tensor_tensor(lg[0:E1, 1, 0:C], lg[0:E1, 1, 0:C], alpha[0:E1, :],
                                                M01[0:E1, 1, :], ALU.mult, ALU.mult))
                    step(v.tensor_tensor(lv, lv, NEG[:, :, :], ALU.add))
                    step(v.tensor_reduce(lmx, lv, AX.X, ALU.max))
                    v.tensor_tensor(lv, lv, lmx.unsqueeze(2).to_broadcast([P, 2, C]),
                                    ALU.subtract).then_inc(s_ls[h], 1)
                    dve.wait_ge(s_le[h], k + 1)
                    step(v.tensor_reduce(lsum, lv, AX.X, ALU.add))
                    step(v.reciprocal(linv, lsum))
                    step(v.tensor_tensor(lg[:, :, C:256], lg[:, :, P:C],
                                         linv.unsqueeze(2).to_broadcast([P, 2, E1]), ALU.mult))
                    v.tensor_tensor(lv, lv, linv.unsqueeze(2).to_broadcast([P, 2, C]),
                                    ALU.mult).then_inc(s_at[h], 1)
                    if k:
                        attention_low(k - 1)
                attention_low(HALF - 1)

            for m in range(NRC * BPC):
                n, hp, t = m // BPC, m // 2 % HALF, m % 2
                if m % BPC == 0:
                    dve.wait_ge(s_xl[n % 3], 32 * (n // 3 + 1))
                rows = E1 if t else P
                dve.wait_ge(s_av, m + 1)
                o = XO[n % 3][0:rows, t, :, hp * 2 * D:(hp + 1) * 2 * D]
                v.scalar_tensor_tensor(o, PS[0:rows, m % 8, :].rearrange("p (r e) -> p r e", r=RI),
                                       mxb[0:rows, WV:WV + 1], o, ALU.mult, ALU.add).then_inc(s_ad, 1)

        @block.tensor
        def _(pe):
            mm = nc.tensor.matmul
            pe.wait_ge(s_const, 4)
            pe.wait_ge(s_wmax, 1)
            nc.tensor.transpose(PS[0:5, 0, 0:P], mx5, ident[:, :]).then_inc(s_wmaxT, 1)
            pe.wait_ge(s_wd, 1)
            mm(PS[:, 1, 0:5], ones[0:5, :], d5[0:5, :], start=True, stop=True).then_inc(s_wb, 1)
            pe.wait_ge(s_wsc, 1)
            nc.tensor.transpose(PS[:, 2, 0:P], W[:, WKS, 0, 0:P], ident[:, :])
            nc.tensor.transpose(PS[:, 2, P:E], W[0:E1, WKS, 1, 0:P], ident[0:E1, 0:E1])
            nc.tensor.transpose(PS[:, 2, E:256], W[0:E1, WKS, 0, 0:P], ident[0:E1, 0:E1])
            nc.tensor.transpose(PS[0:E1, 2, 256:384], W[:, WKS, 0, P:E], ident[:, :])
            nc.tensor.transpose(PS[0:E1, 2, 384:448], W[0:E1, WKS, 1, P:E], ident[0:E1, 0:E1])
            nc.tensor.transpose(PS[0:E1, 2, 448:512], W[0:E1, WKS, 0, P:E], ident[0:E1, 0:E1])
            nc.tensor.transpose(PS[:, 6, 0:P], X0[:, 0, 0:P], ident[:, :])
            nc.tensor.transpose(PS[:, 6, P:C], X0[0:E1, 1, 0:P], ident[0:E1, 0:E1])
            nc.tensor.transpose(PS[0:E1, 6, C:C + P], X0[:, 0, P:E], ident[:, :])
            nc.tensor.transpose(PS[0:E1, 6, C + P:2 * C], X0[0:E1, 1, P:E], ident[0:E1, 0:E1]).then_inc(s_wkt, 1)
            pe.wait_ge(s_st1, 1)
            mm(PS[:, 1, 0:G], ones[:, :], s1, start=True, stop=True).then_inc(s_mm1, 1)
            pe.wait_ge(s_st2, 1)
            mm(PS[:, 0, 0:G], ones[:, :], s2, start=True, stop=True).then_inc(s_mm2, 1)
            pe.wait_ge(s_ab, 1)
            for k in range(2):
                for t, e0 in enumerate((0, P, E1)):
                    ins = mm(PS[:, 7, 3 * k + t:3 * k + t + 1], AB[0:1, k, e0:e0 + P],
                             ones[0:1, 0:1], start=True, stop=True)
            ins.then_inc(s_abT, 1)

            def row_queries():
                pe.wait_ge(s_x0n, 1)
                for m, (lo, n) in enumerate(((0, P), (P, E1))):
                    po = PS[0:n, 7, m * C:(m + 1) * C]
                    mm(po, W[:, WQS, 0, lo:lo + n], QX[:, 0, :], start=True, stop=False)
                    ins = mm(po, W[0:E1, WQS, 1, lo:lo + n], QX[0:E1, 1, :], start=False, stop=True)
                ins.then_inc(s_qs, 1)

            def score_vectors(k):
                pe.wait_ge(s_qm, 1)
                when(pe, s_ul, k)
                for hd in (2 * k, 2 * k + 1):
                    t, row, par = hd // 8, 32 * ((hd % 8) // 2), hd % 2
                    for o, n, e0, cols in ((0, C // 2, 0, QM[row:row + 32, t, par, 0:C:2]),
                                           (C // 2, C // 2, E1, QM[row:row + 32, t, par, 1:C:2]),
                                           (C, C, P, QM[row:row + 32, t, par, :])):
                        ins = mm(PS[:, 6 + par, o:o + n], WKT[row:row + 32, t, e0:e0 + P], cols,
                                 start=True, stop=True)
                ins.then_inc(s_u, 1)

            def scores(m):
                pe.wait_ge(s_l, 2 * m + 2)
                pe.wait_ge(s_ld, 2 * m + 2)
                pe.wait_ge(s_ul, len(U_AT))
                when(pe, s_se, m - 1)
                first = True
                for q in range(CI):
                    j = m * CI + q
                    tt, q2 = TT[2 * m + q // (CI // 2)], q % (CI // 2)
                    for a in range(2):
                        for s, u in ((0, UH0), (0, UL0), (1, UH0)):
                            mm(PS[:, 6 + m % 2, (2 * q + a) * H:(2 * q + a + 1) * H],
                               tt[:, 2 * a, s, q2 * P:(q2 + 1) * P],
                               u[:, (a * C // 2 + j) * H:(a * C // 2 + j + 1) * H],
                               start=first, stop=False, skip_group_check=True)
                            first = False
                    for s, u in ((0, UH1), (0, UL1), (1, UH1)):
                        ins = mm(PS[:, 6 + m % 2, 2 * q * H:(2 * q + 2) * H], tt[:, 1, s, q2 * P:(q2 + 1) * P],
                                 u[:, j * 2 * H:(j + 1) * 2 * H], start=False, stop=True,
                                 skip_group_check=True)
                ins.then_inc(s_sc, 1)

            for c in range(NCH):
                b = c % 2
                when(pe, s_xn, c - 1)
                when(pe, s_xc, c - 1)
                for q in range(CI // 2):
                    for k in range(3):
                        at = (c * CI + 2 * q) * E + k * P
                        ins = nc.tensor.transpose(PS[:, 3 * b + k, q * P:(q + 1) * P], X[:, at:at + P],
                                                  ident[:, :])
                ins.then_inc(s_tr, 1)
                if c == 0:
                    row_queries()
                if c in U_AT:
                    score_vectors(U_AT.index(c))
                for k in scored_at[c]:
                    scores(k)

            def part_transposes(p, src):
                for k in range(BLOCKS):
                    ins = nc.tensor.transpose(part_psum(p)[:, k * P:(k + 1) * P],
                                              src[:, (p * BLOCKS + k) * P:(p * BLOCKS + k + 1) * P], ident[:, :])
                return ins

            for p in range(PARTS):
                pe.wait_ge(s_xn, NCH if p else NCH - 1)
                pe.wait_ge(s_xc, NCH if p else NCH - 1)
                pe.wait_ge(s_se, PAIRS * (p + 1))
                part_transposes(p, SW).then_inc(s_stt, 1)
                if p < len(scored_at[NCH]):
                    scores(scored_at[NCH][p])
            for p in range(PARTS):
                pe.wait_ge(s_snm, p + 1)
                part_transposes(p, FLAT).then_inc(s_swt, 1)

            pe.wait_ge(s_wl, len(W_PARTS))
            for h in range(2):
                wc = slice(h * CW[0], h * CW[0] + CW[h])

                def body(t):
                    for g in range(SPT[h]):
                        n = SPT[h] * t + g
                        b, at = divmod(g * SI[h], CI)
                        if at == 0:
                            pe.wait_ge(s_xt[h][b], 32 * (t + 1))
                        when(pe, s_kvl[h], n - 3)
                        if h == 0 and isinstance(t, int) and g < PARTS:
                            pe.wait_ge(s_sw, g + 1)
                        ps = projected(h, g)
                        for i in range(SI[h]):
                            il = at + i
                            po = ps[:, i, 0:CW[h]]
                            slot = (il % 2) * (CI // 2) + il // 2
                            xh0 = XT[b][:, slot * R:(slot + 1) * R]
                            xl0 = XT[b][:, (CI + slot) * R:(CI + slot + 1) * R]
                            x1 = XT[b][:, (2 * CI + slot) * R:(2 * CI + slot + 1) * R]
                            mm(po, xh0, WP[:, 0, 0, wc], start=True, stop=False)
                            mm(po, xh0, WP[:, 1, 0, wc], start=False, stop=False)
                            mm(po, xl0, WP[:, 0, 0, wc], start=False, stop=False)
                            mm(po, x1, WP[:, 0, 1, wc], start=False, stop=False)
                            ins = mm(po, x1, WP[:, 1, 1, wc], start=False, stop=True)
                        ins.then_inc(s_pj[h], 1)

                body(0)
                with pe.Fori(1, TURNS[h]) as t:
                    body(t)

                def transposes(k):
                    lg = LG[k % 2]
                    pe.wait_ge(s_at[h], k + 1)
                    when(pe, s_atl[h], k - 1)
                    pb = PS[:, 4 + k % 2, :]
                    nc.tensor.transpose(pb[:, 0:P], lg[:, 0, 0:P], ident[:, :])
                    nc.tensor.transpose(pb[:, P:C], lg[0:E1, 1, 0:P], ident[0:E1, 0:E1])
                    nc.tensor.transpose(pb[:, C:C + P], lg[:, 0, P:256], ident[:, :])
                    nc.tensor.transpose(pb[:, C + P:2 * C], lg[0:E1, 1, P:256],
                                        ident[0:E1, 0:E1]).then_inc(s_att[h], 1)

                pe.wait_ge(s_ql[h], NG[h])
                pe.wait_ge(s_kvl[h], NG[h])
                for k in range(HALF):
                    when(pe, s_lr[h], k - 1)
                    for d in range(D):
                        m = k * D + d
                        first, last = d == 0, d == D - 1
                        p0, p1 = PS[:, 2 * (k % 2), 0:C], PS[:, 2 * (k % 2) + 1, 0:C]
                        kh, kl = KA[:, m, 0:C], KA[:, m, C:2 * C]
                        mm(p0, QA[:, m, 0:P], kh, start=first, stop=False)
                        mm(p0, QA[:, m, 0:P], kl, start=False, stop=False)
                        mm(p0, QA[:, m, 2 * P:3 * P], kh, start=False, stop=last)
                        mm(p1, QA[:, m, P:2 * P], kh, start=first, stop=False)
                        ins = mm(p1, QA[:, m, P:2 * P], kl, start=False, stop=last)
                    ins.then_inc(s_qk[h], 1)
                    if k:
                        transposes(k - 1)
                transposes(HALF - 1)

                pe.wait_ge(s_atl[h], HALF)

            for m in range(NRC * BPC):
                n, hp, t = m // BPC, m // 2 % HALF, m % 2
                if m % BPC == 0:
                    pe.wait_ge(s_vl[n % NV], 32 * (n // NV + 1))
                when(pe, s_ad, m - 7)
                if t:
                    when(pe, s_ol, (m - 7) // 2)
                po = PS[:, m % 8, :].rearrange("p (r a d) -> p r a d", a=2, d=D)
                for a in range(2):
                    k = 2 * hp + a
                    at = AT[k // HALF][:, k % HALF, :, :]
                    vb = BUF[n % NV]
                    v0, v1 = V0[vb][:, :, :, k * D:(k + 1) * D], V1[vb][:, :, k * D:(k + 1) * D]
                    if t == 0:
                        high, low = slice(0, P), slice(C + E1, 2 * C)
                        terms = ((at[:, 0, high], v0[:, :, 0, :]), (at[:, 0, high], v0[:, :, 1, :]),
                                 (at[:, 0, low], v0[:, :, 0, :]), (at[:, 1, high], v1), (at[:, 1, low], v1))
                    else:
                        both = slice(P, 2 * P)
                        terms = ((at[:, 0, both], v0[:, :, 0, :]), (at[:, 0, both], v0[:, :, 1, :]),
                                 (at[:, 1, both], v1))
                    for j, (stationary, moving) in enumerate(terms):
                        ins = mm(po[:, :, a, :], stationary, moving, start=j == 0, stop=j == len(terms) - 1)
                ins.then_inc(s_av, 1)


_INS = ["x", "L0_conv_Wq", "L0_conv_Wk", "L0_conv_Wv", "L0_conv_Wq_s", "L0_conv_Wk_s",
        "L0_conv_res_mask", "L0_conv_seq_mask"]


def kernel(**inputs):
    import numpy as _np
    import concourse.bacc as _bacc
    from concourse import mybir as _mybir
    from concourse.bass_utils import run_bass_kernel_spmd as _run

    nc = _bacc.Bacc("TRN2", target_bir_lowering=False, num_devices=1)
    arrays, args = {}, []
    for name in _INS:
        a = _np.ascontiguousarray(inputs[name])
        arrays[f"in_{name}"] = a
        args.append(nc.dram_tensor(f"in_{name}", a.shape, _mybir.dt.from_np(a.dtype), kind="ExternalInput").ap())
    args.append(nc.dram_tensor("out_x", (1, R, C, E), _mybir.dt.float32, kind="ExternalOutput").ap())
    row_column_attention(nc, *args)
    r = _run(nc, [arrays], core_ids=[0])
    return r.results[0]["out_x"]
```
